# Optimizing a Trainium2 kernel written in Bass

```python
import numpy as np
import jax
import jax.numpy as jnp

def _softmax(x, axis=-1):
    return jax.nn.softmax(x, axis=axis)

def _gelu(x):
    return jax.nn.gelu(x, approximate=True)

def _silu(x):
    return jax.nn.silu(x)

def _sigmoid(x):
    return jax.nn.sigmoid(x)

def _layernorm(x, axis=-1, eps=1e-05):
    m = jnp.mean(x, axis=axis, keepdims=True)
    v = jnp.var(x, axis=axis, keepdims=True)
    return (x - m) / jnp.sqrt(v + eps)

def _scatter_add(tgt, idx, src, axis=0):
    return tgt.at[idx].add(src)

def _segment_sum(src, seg, n):
    return jax.ops.segment_sum(src, seg, n)
kernel_name = 'mk_macaron_d1_jaxref_r8_b5c540'

def setup_inputs(seed: int=0):
    np.random.seed(seed)
    _w = jnp.asarray

    def _L0_attn_setup():
        import jax, jax.numpy as jnp
        import numpy as np
        B_SZ, L, D_MODEL = (4, 128, 128)
        D_INNER, D_STATE, D_CONV, DT_RANK = (256, 16, 4, 64)

        def _mamba_fwd(hidden_states, in_proj_w, conv_w, conv_b, x_proj_w, dt_proj_w, dt_bias, A_log, D_param, out_proj_w):
            seqlen = hidden_states.shape[1]
            xz = hidden_states @ in_proj_w
            x, z = jnp.split(xz, 2, axis=-1)
            xpad = jnp.pad(x, ((0, 0), (D_CONV - 1, 0), (0, 0)))
            xc = conv_b
            acc = jnp.zeros_like(x)
            for k in range(D_CONV):
                acc = acc + conv_w[:, k] * xpad[:, k:k + seqlen, :]
            x = jax.nn.silu(acc + conv_b)
            x_dbl = x @ x_proj_w
            dt_low, Bm, Cm = jnp.split(x_dbl, [DT_RANK, DT_RANK + D_STATE], axis=-1)
            dt = jax.nn.softplus(dt_low @ dt_proj_w + dt_bias)
            A = -jnp.exp(A_log)

            def step(h, inp):
                u_t, dt_t, B_t, C_t = inp
                dA = jnp.exp(dt_t[:, :, None] * A)
                dBu = dt_t[:, :, None] * B_t[:, None, :] * u_t[:, :, None]
                h = dA * h + dBu
                y_t = jnp.einsum('bdn,bn->bd', h, C_t)
                return (h, y_t)
            xs = (jnp.swapaxes(x, 0, 1), jnp.swapaxes(dt, 0, 1), jnp.swapaxes(Bm, 0, 1), jnp.swapaxes(Cm, 0, 1))
            h0 = jnp.zeros((x.shape[0], D_INNER, D_STATE), dtype=x.dtype)
            _, y = jax.lax.scan(step, h0, xs)
            y = jnp.swapaxes(y, 0, 1) + D_param * x
            y = y * jax.nn.silu(z)
            return y @ out_proj_w
        key = jax.random.key(seed)
        ks = jax.random.split(key, 9)
        s = 0.02
        hidden_states = jax.random.normal(ks[0], (B_SZ, L, D_MODEL), dtype=jnp.float32)
        in_proj_w = jax.random.normal(ks[1], (D_MODEL, 2 * D_INNER), dtype=jnp.float32) * s
        conv_w = jax.random.normal(ks[2], (D_INNER, D_CONV), dtype=jnp.float32) * 0.3
        conv_b = jax.random.normal(ks[3], (D_INNER,), dtype=jnp.float32) * 0.01
        x_proj_w = jax.random.normal(ks[4], (D_INNER, DT_RANK + 2 * D_STATE), dtype=jnp.float32) * s
        dt_proj_w = jax.random.normal(ks[5], (DT_RANK, D_INNER), dtype=jnp.float32) * DT_RANK ** (-0.5)
        dt = jnp.exp(jax.random.uniform(ks[6], (D_INNER,)) * (np.log(0.1) - np.log(0.001)) + np.log(0.001))
        dt = jnp.clip(dt, 0.0001, None)
        dt_bias = dt + jnp.log(-jnp.expm1(-dt))
        A_log = jnp.log(jnp.broadcast_to(jnp.arange(1, D_STATE + 1, dtype=jnp.float32), (D_INNER, D_STATE)))
        D_param = jnp.ones((D_INNER,), dtype=jnp.float32)
        out_proj_w = jax.random.normal(ks[7], (D_INNER, D_MODEL), dtype=jnp.float32) * s
        return {'hidden_states': hidden_states, 'in_proj_w': in_proj_w, 'conv_w': conv_w, 'conv_b': conv_b, 'x_proj_w': x_proj_w, 'dt_proj_w': dt_proj_w, 'dt_bias': dt_bias, 'A_log': A_log, 'D_param': D_param, 'out_proj_w': out_proj_w}
    _L0_attn_in = _L0_attn_setup()

    def _L0_ffn_setup():
        import jax, jax.numpy as jnp
        import numpy as np
        B, S, D = (2, 256, 128)
        E, K, DFF = (8, 2, 4 * 128)
        EPS_GATE = 1e-08
        EPS_LN = 1e-05
        key = jax.random.key(seed)
        ks = jax.random.split(key, 4)
        scaled = lambda k, shape, fan: jax.random.normal(k, shape, jnp.float32) / np.sqrt(fan).astype(np.float32)
        return {'x': jax.random.normal(ks[0], (B, S, D), jnp.float32), 'Wg': scaled(ks[1], (D, E), D), 'bg': jnp.zeros((E,), jnp.float32), 'W1': scaled(ks[2], (E, D, DFF), D), 'b1': jnp.zeros((E, DFF), jnp.float32), 'W2': scaled(ks[3], (E, DFF, D), DFF), 'b2': jnp.zeros((E, D), jnp.float32), 'gamma': jnp.ones((D,), jnp.float32), 'beta': jnp.zeros((D,), jnp.float32)}
    _L0_ffn_in = _L0_ffn_setup()
    _d = {'L0_attn_hidden_states': _L0_attn_in['hidden_states'], 'L0_attn_in_proj_w': _L0_attn_in['in_proj_w'], 'L0_attn_conv_w': _L0_attn_in['conv_w'], 'L0_attn_conv_b': _L0_attn_in['conv_b'], 'L0_attn_x_proj_w': _L0_attn_in['x_proj_w'], 'L0_attn_dt_proj_w': _L0_attn_in['dt_proj_w'], 'L0_attn_dt_bias': _L0_attn_in['dt_bias'], 'L0_attn_A_log': _L0_attn_in['A_log'], 'L0_attn_D_param': _L0_attn_in['D_param'], 'L0_attn_out_proj_w': _L0_attn_in['out_proj_w'], 'L0_ffn_Wg': _L0_ffn_in['Wg'], 'L0_ffn_bg': _L0_ffn_in['bg'], 'L0_ffn_W1': _L0_ffn_in['W1'], 'L0_ffn_b1': _L0_ffn_in['b1'], 'L0_ffn_W2': _L0_ffn_in['W2'], 'L0_ffn_b2': _L0_ffn_in['b2'], 'L0_ffn_gamma': _L0_ffn_in['gamma'], 'L0_ffn_beta': _L0_ffn_in['beta']}
    _x0 = _d['L0_attn_hidden_states']
    _d['L0_attn_hidden_states'] = jax.random.normal(jax.random.fold_in(jax.random.key(seed), 1), (2, 1024, 128), dtype=_x0.dtype)
    del _x0
    return _d

def reference(L0_attn_hidden_states, L0_attn_in_proj_w, L0_attn_conv_w, L0_attn_conv_b, L0_attn_x_proj_w, L0_attn_dt_proj_w, L0_attn_dt_bias, L0_attn_A_log, L0_attn_D_param, L0_attn_out_proj_w, L0_ffn_Wg, L0_ffn_bg, L0_ffn_W1, L0_ffn_b1, L0_ffn_W2, L0_ffn_b2, L0_ffn_gamma, L0_ffn_beta):

    def _L0_attn_ref(hidden_states, in_proj_w, conv_w, conv_b, x_proj_w, dt_proj_w, dt_bias, A_log, D_param, out_proj_w):
        import jax, jax.numpy as jnp
        import numpy as np
        B_SZ, L, D_MODEL = (4, 128, 128)
        D_INNER, D_STATE, D_CONV, DT_RANK = (256, 16, 4, 64)

        def _mamba_fwd(hidden_states, in_proj_w, conv_w, conv_b, x_proj_w, dt_proj_w, dt_bias, A_log, D_param, out_proj_w):
            seqlen = hidden_states.shape[1]
            xz = hidden_states @ in_proj_w
            x, z = jnp.split(xz, 2, axis=-1)
            xpad = jnp.pad(x, ((0, 0), (D_CONV - 1, 0), (0, 0)))
            xc = conv_b
            acc = jnp.zeros_like(x)
            for k in range(D_CONV):
                acc = acc + conv_w[:, k] * xpad[:, k:k + seqlen, :]
            x = jax.nn.silu(acc + conv_b)
            x_dbl = x @ x_proj_w
            dt_low, Bm, Cm = jnp.split(x_dbl, [DT_RANK, DT_RANK + D_STATE], axis=-1)
            dt = jax.nn.softplus(dt_low @ dt_proj_w + dt_bias)
            A = -jnp.exp(A_log)

            def step(h, inp):
                u_t, dt_t, B_t, C_t = inp
                dA = jnp.exp(dt_t[:, :, None] * A)
                dBu = dt_t[:, :, None] * B_t[:, None, :] * u_t[:, :, None]
                h = dA * h + dBu
                y_t = jnp.einsum('bdn,bn->bd', h, C_t)
                return (h, y_t)
            xs = (jnp.swapaxes(x, 0, 1), jnp.swapaxes(dt, 0, 1), jnp.swapaxes(Bm, 0, 1), jnp.swapaxes(Cm, 0, 1))
            h0 = jnp.zeros((x.shape[0], D_INNER, D_STATE), dtype=x.dtype)
            _, y = jax.lax.scan(step, h0, xs)
            y = jnp.swapaxes(y, 0, 1) + D_param * x
            y = y * jax.nn.silu(z)
            return y @ out_proj_w
        return _mamba_fwd(hidden_states, in_proj_w, conv_w, conv_b, x_proj_w, dt_proj_w, dt_bias, A_log, D_param, out_proj_w)

    def _L0_ffn_ref(x, Wg, bg, W1, b1, W2, b2, gamma, beta):
        import jax, jax.numpy as jnp
        import numpy as np
        B, S, D = (2, 256, 128)
        E, K, DFF = (8, 2, 4 * 128)
        EPS_GATE = 1e-08
        EPS_LN = 1e-05
        b, s, d = x.shape
        xf = x.reshape(-1, d)
        T = xf.shape[0]
        num_experts = Wg.shape[1]
        logits = xf @ Wg + bg
        w = jax.nn.softmax(logits, axis=-1)
        top_w, top_idx = jax.lax.top_k(w, K)
        top_w = top_w / (top_w.sum(axis=-1, keepdims=True) + EPS_GATE)
        cw = jnp.zeros((T, num_experts), xf.dtype).at[jnp.arange(T)[:, None], top_idx].add(top_w)
        out = jnp.zeros_like(xf)
        for e in range(num_experts):
            h = jax.nn.gelu(xf @ W1[e] + b1[e], approximate=False)
            y = h @ W2[e] + b2[e]
            out = out + cw[:, e:e + 1] * y
        mu = out.mean(axis=-1, keepdims=True)
        var = out.var(axis=-1, keepdims=True)
        out = (out - mu) / jnp.sqrt(var + EPS_LN) * gamma + beta
        return out.reshape(b, s, d)
    x = L0_attn_hidden_states
    x = x + 0.5 * _L0_ffn_ref(_layernorm(x, axis=-1), L0_ffn_Wg, L0_ffn_bg, L0_ffn_W1, L0_ffn_b1, L0_ffn_W2, L0_ffn_b2, L0_ffn_gamma, L0_ffn_beta)
    x = x + _L0_attn_ref(_layernorm(x, axis=-1), L0_attn_in_proj_w, L0_attn_conv_w, L0_attn_conv_b, L0_attn_x_proj_w, L0_attn_dt_proj_w, L0_attn_dt_bias, L0_attn_A_log, L0_attn_D_param, L0_attn_out_proj_w)
    x = x + 0.5 * _L0_ffn_ref(_layernorm(x, axis=-1), L0_ffn_Wg, L0_ffn_bg, L0_ffn_W1, L0_ffn_b1, L0_ffn_W2, L0_ffn_b2, L0_ffn_gamma, L0_ffn_beta)
    return x

_drawn_inputs = setup_inputs


def setup_inputs(seed=0):
    import zlib

    import numpy as np

    out = dict(_drawn_inputs(seed))
    spreads = {'L0_attn_D_param': (1.0, 0.6),
     'L0_ffn_bg': (0.0, 0.1),
     'L0_ffn_b1': (0.0, 0.1),
     'L0_ffn_b2': (0.0, 0.1),
     'L0_ffn_gamma': (1.0, 0.2),
     'L0_ffn_beta': (0.0, 0.1)}
    factors = {'L0_attn_in_proj_w': 3.539,
     'L0_attn_conv_w': 3.743,
     'L0_attn_conv_b': 8.0,
     'L0_attn_x_proj_w': 8.0,
     'L0_attn_dt_proj_w': 8.0,
     'L0_attn_dt_bias': 8.0,
     'L0_attn_A_log': 8.0,
     'L0_attn_out_proj_w': 3.788}
    for name, (base, spread) in spreads.items():
        noise = np.random.default_rng([zlib.crc32(name.encode()), seed]).standard_normal(out[name].shape)
        drawn = base * np.exp(spread * noise) if base else spread * noise
        out[name] = jnp.asarray(drawn.astype(out[name].dtype))
    for name, factor in factors.items():
        out[name] = (out[name] * factor).astype(out[name].dtype)
    return out
```

```python
from contextlib import ExitStack

import concourse.bass as bass
from concourse import mybir

F32 = mybir.dt.float32
F32R = mybir.dt.float32r
ALU = mybir.AluOpType
ACT = mybir.ActivationFunctionType
AX = mybir.AxisListType.X

P = 128
CT = 256
TT = CT // P
LAG = 4
EPS_LN = 1e-5
EPS_GATE = 1e-8
FAR = -3.0e38
NSLOT = 8
WB = 3
BB = 3
HALF_LN2 = 0.34657359027997264
ATANH = (2.000000007877748, 0.6666631593508229, 0.4002485372340695, 0.27961418835789853, 0.28174657258139)


def wait(eng, sem, value):
    if isinstance(value, int) and value <= 0:
        return
    eng.wait_ge(sem, value)


def macaron(nc, hidden, in_w, conv_w, conv_b, xp_w, dt_w, dt_b, a_log, d_par, out_w,
            Wg, bg, W1, b1, W2, b2, gamma, beta, cw_dram, out):
    NB, L, D = hidden.shape
    E, _, DFF = W1.shape
    M = DFF // P
    DI = in_w.shape[1] // 2
    H = DI // P
    NS = a_log.shape[1]
    KC = conv_w.shape[1]
    R = dt_w.shape[0]
    CHUNKS = NB * L // CT
    NT = CHUNKS * TT
    UNITS = CHUNKS + LAG
    LOOP = (LAG + 1, CHUNKS - 1)
    WORK = E * M + E
    ADDS = E - 1
    NB1 = E * M
    ROWS = NB1 + 3 * H

    with ExitStack() as ctx:
        def sb(name, shape, dt=F32):
            return ctx.enter_context(nc.sbuf_tensor(name, shape, dt))

        def sem(name):
            return ctx.enter_context(nc.semaphore(name))

        def flat(ap):
            return ap.rearrange("p a b -> p (a b)")

        w1_hi = sb("w1_hi", [P, E, DFF], F32R)
        w1_lo = sb("w1_lo", [P, E, DFF], F32R)
        w2 = sb("w2", [P, E, M, D])
        wg_hi = sb("wg_hi", [P, E], F32R)
        wg_lo = sb("wg_lo", [P, E], F32R)
        win_hi = sb("win_hi", [P, 2 * DI], F32R)
        win_lo = sb("win_lo", [P, 2 * DI], F32R)
        xp_sb = sb("xp_sb", [P, H, R + 2 * NS])
        dtw_sb = sb("dtw_sb", [R, DI])
        wout_sb = sb("wout_sb", [P, H, D])
        b2_sb = sb("b2_sb", [E, D])
        gamma_h = sb("gamma_h", [P, D])
        beta_h = sb("beta_h", [P, D])
        bg_sb = sb("bg_sb", [P, E])
        cols = sb("cols", [P, ROWS])
        convw_sb = sb("convw_sb", [P, H, KC])
        a_neg = sb("a_neg", [P, H, NS])
        ident = sb("ident", [P, P])
        pick = sb("pick", [2 * 2 * NS, 2 * NS], F32R)
        euler = sb("euler", [P, 2 * TT, E])
        mhalf = sb("mhalf", [P, 2 * TT])
        rank = sb("rank", [P, 2 * TT, E])
        b1_col = cols[:, 0:NB1]
        convb_col = cols[:, NB1:NB1 + H]
        dtb_col = cols[:, NB1 + H:NB1 + 2 * H]
        dpar_col = cols[:, NB1 + 2 * H:ROWS]

        xs = sb("xs", [P, NT, D])
        hid = sb("hid", [P, E * M, 2 * CT])
        rows = hid[0:ROWS, E + 2, 0:P]
        cwB = sb("cwB", [P, E, 2 * CT])
        cwT = sb("cwT", [E, 2 * CT])
        xn = sb("xn", [P, 2 * TT, D])
        x_hi = sb("x_hi", [P, 2 * CT], F32R)
        x_lo = sb("x_lo", [P, 2 * CT], F32R)
        gated = sb("gated", [P, 2, 2 * CT])
        acc = sb("acc", [P, 2 * CT])
        on = xn
        f_st = sb("f_st", [P, 2 * TT, 6])
        f_mv = sb("f_mv", [P, 2 * TT, 2])
        f_ve = sb("f_ve", [P, 2 * TT])
        f_rs = sb("f_rs", [P, 2 * TT])
        o_st = sb("o_st", [P, 2 * TT, 6])
        o_mv = sb("o_mv", [P, 2 * TT, 2])
        o_ve = sb("o_ve", [P, 2 * TT])
        o_rs = sb("o_rs", [P, 2 * TT])
        lg = sb("lg", [P, 2 * TT, E])
        lg2 = sb("lg2", [P, 2 * TT, E])
        sh = sb("sh", [P, 2 * TT, E])
        ex = sb("ex", [P, 2 * TT, E])
        num = lg2
        cw = sb("cw", [P, 2 * TT, E])
        eq = sb("eq", [P, 2 * TT, E])
        first = sb("first", [P, 2 * TT, E])
        both = sb("both", [P, 2 * TT, E])
        top = sb("top", [P, 2 * TT])
        best = sb("best", [P, 2 * TT])
        whole = sb("whole", [P, 2 * TT])
        den = sb("den", [P, 2 * TT])
        spare = sb("spare", [P, 1])
        half_ln2 = sb("half_ln2", [P, 1])

        xm = sb("xm", [P, TT, D])
        xm_hi = sb("xm_hi", [P, CT], F32R)
        xm_lo = sb("xm_lo", [P, CT], F32R)
        m_st = sb("m_st", [P, TT, 6])
        m_mv = sb("m_mv", [P, TT, 2])
        m_ve = sb("m_ve", [P, TT])
        m_rs = sb("m_rs", [P, TT])
        xpad = sb("xpad", [P, H, KC - 1 + CT])
        halo = sb("halo", [P, 2, H, KC - 1])
        u = sb("u", [P, H, CT])
        zs_next = sb("zs_next", [P, H, CT])
        tanh = gated[:, 0].rearrange("p (h t) -> p h t", h=H)
        zs = sb("zs", [P, H, CT])
        dt_low = flat(xm[:, :, :])[0:R]
        bc = sb("bc", [4 * NS, CT], F32R)
        dt = sb("dt", [P, H, CT])
        dtu = sb("dtu", [P, H, CT])
        decay = sb("decay", [P, NSLOT, H, CT])
        drive = sb("drive", [P, 2, H, CT])
        state = sb("state", [P, 2, H, CT])
        seen = sb("seen", [P, 2, H, CT])
        y_acc = sb("y_acc", [P, H, CT])
        carry = sb("carry", [P, 2, H, NS])
        carry_new = sb("carry_new", [P, H, NS])

        sp_abs, sp_exp, sp_s4 = drive[:, 0], seen[:, 1], seen[:, 0]
        sp_poly, sp_pos = state[:, 0], state[:, 1]
        sp_sq, sp_tanh = drive[:, 1], state[:, 0]

        work = [ctx.enter_context(nc.psum_tensor(f"work{i}", [P, 512], F32)) for i in range(WB)]
        f_bank = ctx.enter_context(nc.psum_tensor("f_bank", [P, 512], F32))
        m_bank = ctx.enter_context(nc.psum_tensor("m_bank", [P, 512], F32))
        bc_bank = [ctx.enter_context(nc.psum_tensor(f"bc_bank{i}", [P, 512], F32)) for i in range(BB)]

        ld_x = sem("ld_x")
        ld_w1 = [sem(f"ld_w1_{e}") for e in range(E)]
        ld_w2 = sem("ld_w2")
        ld_vec = sem("ld_vec")
        ld_mamba = sem("ld_mamba")
        consts_made = sem("consts_made")
        ident_made = sem("ident_made")
        pool_setup = sem("pool_setup")
        split_made = sem("split_made")
        cols_turned = sem("cols_turned")
        cols_made = sem("cols_made")
        a_exp = sem("a_exp")
        scaled = sem("scaled")
        ln_f = sem("ln_f")
        rstd_f = sem("rstd_f")
        x_turned = sem("x_turned")
        x_split = sem("x_split")
        logits_made = sem("logits_made")
        route = sem("route")
        powers = sem("powers")
        cw_turned = sem("cw_turned")
        cwT_made = sem("cwT_made")
        cw_stored = sem("cw_stored")
        cw_spread = sem("cw_spread")
        work_full = sem("work_full")
        gelu_done = sem("gelu_done")
        gate_done = sem("gate_done")
        acc_added = sem("acc_added")
        out_turned = sem("out_turned")
        ln_o = sem("ln_o")
        rstd_o = sem("rstd_o")
        affine = sem("affine")
        ffn1_added = sem("ffn1_added")
        ffn2_added = sem("ffn2_added")
        stored = sem("stored")
        ln_m = sem("ln_m")
        rstd_m = sem("rstd_m")
        xm_turned = sem("xm_turned")
        xm_split = sem("xm_split")
        inx_made = sem("inx_made")
        inz_made = sem("inz_made")
        xpad_made = sem("xpad_made")
        halo_set = sem("halo_set")
        z_read = sem("z_read")
        conv = sem("conv")
        x_tanh = sem("x_tanh")
        silu = sem("silu")
        xdbl_made = sem("xdbl_made")
        xdbl_read = sem("xdbl_read")
        dt_made = sem("dt_made")
        dt_read = sem("dt_read")
        sp_act = sem("sp_act")
        sp_dve = sem("sp_dve")
        begun = sem("begun")
        bc_spread = sem("bc_spread")
        decay_made = sem("decay_made")
        drive_made = sem("drive_made")
        scanned = sem("scanned")
        seen_made = sem("seen_made")
        y_added = sem("y_added")
        carry_kept = sem("carry_kept")
        carry_moved = sem("carry_moved")
        y_gated = sem("y_gated")
        mamba_made = sem("mamba_made")
        mamba_added = sem("mamba_added")

        N_OF = {0: [], 1: [], 2: [0], 3: [1], 4: [2, 3], 5: [4, 5], 6: [6, 7], 7: [8]}
        N_A = 9
        ROUTE = 20
        SPD = 8

        def parts(k):
            if not isinstance(k, int):
                return True, True
            return 0 <= k < CHUNKS, LAG <= k < UNITS

        def span(k):
            f1, f2 = parts(k)
            return (0 if f1 else TT), (2 * TT if f2 else TT)

        def chunk_ok(c):
            return not isinstance(c, int) or 0 <= c < CHUNKS

        def unit_ok(k):
            return not isinstance(k, int) or 0 <= k < UNITS

        def x_tile(k, j):
            at = TT * k + j if j < TT else TT * (k - LAG) + j - TT
            return xs[:, at, :] if isinstance(at, int) else xs[:, bass.ds(at, 1), :].rearrange("p a d -> p (a d)")

        def x_chunk(c):
            at = TT * c
            return xs[:, at:at + TT, :] if isinstance(at, int) else xs[:, bass.ds(at, TT), :]

        def over_units(eng, body):
            for k in range(LOOP[0]):
                body(k)
            with eng.Fori(*LOOP) as k:
                body(k)
            for k in range(LOOP[1], UNITS + 1):
                body(k)

        block = ctx.enter_context(nc.Block())

        @block.sync
        def _(sp):
            for b in range(NB):
                for r in range(TT):
                    dst = xs[:, :, :].rearrange("p (q b r) d -> p q b r d", b=NB, r=TT)[:, :, b, r]
                    src = hidden[b].rearrange("(q r p) d -> p q r d", p=P, r=TT)[:, :, r]
                    sp.dma_start(dst, src).then_inc(ld_x, 16)
            sp.dma_start(rows[0:NB1, :], b1.rearrange("e (m p) -> (e m) p", p=P)).then_inc(ld_vec, 16)
            for i, v in enumerate((conv_b, dt_b, d_par)):
                sp.dma_start(rows[NB1 + H * i:NB1 + H * i + H, :],
                             v.rearrange("(h p) -> h p", p=P)).then_inc(ld_vec, 16)
            sp.dma_start(bg_sb[:, :], bg.rearrange("(a e) -> a e", a=1).to_broadcast([P, E])).then_inc(ld_vec, 16)
            sp.dma_start(hid[:, E, 0:E], Wg).then_inc(ld_vec, 16)
            for e in range(E):
                sp.dma_start(hid[:, e, :], W1[e]).then_inc(ld_w1[e], 16)
            sp.dma_start(hid[:, E + 1, 0:2 * DI], in_w).then_inc(ld_mamba, 16)
            sp.dma_start(xp_sb[:, :, :], xp_w.rearrange("(h p) n -> p h n", p=P)).then_inc(ld_mamba, 16)
            sp.dma_start(dtw_sb[:, :], dt_w).then_inc(ld_mamba, 16)
            sp.dma_start(wout_sb[:, :, :], out_w.rearrange("(h p) n -> p h n", p=P)).then_inc(ld_mamba, 16)

            def gates(k):
                t0, t1 = span(k)
                c0, c1 = t0 * P, t1 * P
                wait(sp, cwT_made, k + 1)
                sp.dma_start(cw_dram[:, c0:c1], cwT[:, c0:c1]).then_inc(cw_stored, 16)
                wait(sp, gate_done, E * k)
                sp.wait_ge(cw_stored, 16 * k + 16)
                src = cw_dram[:, c0:c1].rearrange("(a e) c -> a e c", a=1).to_broadcast([P, E, c1 - c0])
                sp.dma_start(cwB[:, :, c0:c1], src).then_inc(cw_spread, 16)

            def store(q, b):
                rows_out = out[b].rearrange("(q p) d -> p q d", p=P)
                if isinstance(q, int):
                    c = NB * q + b
                    dst, src = rows_out[:, TT * q:TT * q + TT, :], xs[:, TT * c:TT * c + TT, :]
                else:
                    to = sp.snap(TT * q)
                    at = sp.snap(TT * NB * q + TT * b)
                    dst, src = rows_out[:, bass.ds(to, TT), :], xs[:, bass.ds(at, TT), :]
                sp.wait_ge(ffn2_added, NB * q + b + 1)
                sp.dma_start(dst, src).then_inc(stored, 16)

            for k in range(LAG + 1):
                gates(k)
            with sp.Fori(0, (CHUNKS - LAG - 1) // NB) as q:
                for b in range(NB):
                    gates(NB * q + LAG + 1 + b)
                    store(q, b)
            for c in range((CHUNKS - LAG - 1) // NB * NB, CHUNKS):
                if c + LAG + 1 < UNITS:
                    gates(c + LAG + 1)
                store(c // NB, c % NB)
            sp.wait_ge(stored, 16 * CHUNKS)

        @block.gpsimd
        def _(pool):
            g = nc.gpsimd
            g.memset(ident[:, :], 0.0).then_inc(pool_setup, 1)
            pool.wait_ge(pool_setup, 1)
            g.affine_select(out=ident[:, :], in_=ident[:, :], compare_op=ALU.not_equal, fill=1.0, base=0,
                            pattern=[[-1, P]], channel_multiplier=1).then_inc(ident_made, 1)
            g.memset(euler[:, :, :], 2.718281828459045)
            g.memset(mhalf[:, :], -0.5)
            g.memset(half_ln2[:, :], HALF_LN2)
            g.memset(halo[:, :, :, :], 0.0)
            g.memset(carry[:, :, :, :], 0.0).then_inc(pool_setup, 1)
            pool.wait_ge(pool_setup, 2)

            def rstd_unit(k, ve, rs, needed, done):
                t0, t1 = span(k)
                pool.wait_ge(needed, 4 * k + 3)
                g.tensor_tensor(rs[:, t0:t1], ve[:, t0:t1], mhalf[:, t0:t1], ALU.pow).then_inc(done, 1)

            def router(k):
                t0, t1 = span(k)
                pool.wait_ge(route, ROUTE * k + 3)
                g.tensor_tensor(ex[:, t0:t1], euler[:, t0:t1], sh[:, t0:t1], ALU.pow).then_inc(powers, 1)

            def add_state(c, n):
                pool.wait_ge(seen_made, NS * c + n + 1)
                if n == 0:
                    wait(pool, carry_moved, 2 * c)
                    pool.wait_ge(begun, 2 * c + 1)
                else:
                    pool.wait_ge(y_added, NS * c + n)
                g.tensor_tensor(flat(y_acc[:, :, :]), flat(y_acc[:, :, :]), flat(seen[:, n % 2]),
                                ALU.add).then_inc(y_added, 1)
                g.tensor_copy(carry_new[:, :, n:n + 1], state[:, n % 2, :, CT - 1:CT]).then_inc(carry_kept, 1)

            def add_expert(k, e):
                t0, t1 = span(k)
                c0, c1 = t0 * P, t1 * P
                pool.wait_ge(gate_done, E * k + e + 1)
                if e == 1:
                    wait(pool, out_turned, k)
                    g.tensor_tensor(acc[:, c0:c1], gated[:, 0, c0:c1], gated[:, 1, c0:c1], ALU.add).then_inc(acc_added, 1)
                else:
                    pool.wait_ge(acc_added, ADDS * k + e - 1)
                    g.tensor_tensor(acc[:, c0:c1], acc[:, c0:c1], gated[:, e % 2, c0:c1], ALU.add).then_inc(acc_added, 1)

            def out_affine(k):
                t0, t1 = span(k)
                pool.wait_ge(ln_o, 4 * k + 4)
                if k_is0(k):
                    pool.wait_ge(scaled, 2)
                gb = gamma_h[:, :].rearrange("p (a d) -> p a d", a=1).to_broadcast([P, t1 - t0, D])
                bb = beta_h[:, :].rearrange("p (a d) -> p a d", a=1).to_broadcast([P, t1 - t0, D])
                g.tensor_tensor(on[:, t0:t1], on[:, t0:t1], gb, ALU.mult).then_inc(affine, 1)
                pool.wait_ge(affine, 2 * k + 1)
                g.tensor_tensor(on[:, t0:t1], on[:, t0:t1], bb, ALU.add).then_inc(affine, 1)

            def k_is0(k):
                return isinstance(k, int) and k == 0

            def body(k):
                c1, c2, c3 = k - 1, k - 2, k - 3
                for e in range(E):
                    if e == 0 and unit_ok(k) and not k_is0(k):
                        router(k)
                    if e >= 1 and chunk_ok(c3):
                        add_state(c3, N_A + e - 2)
                    if e == 2 and unit_ok(k - 1):
                        rstd_unit(k - 1, o_ve, o_rs, ln_o, rstd_o)
                    if e == 3 and unit_ok(k - 1):
                        out_affine(k - 1)
                    if e == 4 and chunk_ok(c1):
                        pool.wait_ge(ln_m, 4 * c1 + 3)
                        g.tensor_tensor(m_rs[:, :], m_ve[:, :], mhalf[:, 0:TT], ALU.pow).then_inc(rstd_m, 1)
                if chunk_ok(c3):
                    add_state(c3, NS - 1)
                for e in range(E):
                    if e >= 1 and unit_ok(k):
                        add_expert(k, e)
                    if chunk_ok(c2):
                        for n in N_OF[e]:
                            if n >= 1:
                                add_state(c2, n - 1)
                    if e == 3 and unit_ok(k + 1):
                        rstd_unit(k + 1, f_ve, f_rs, ln_f, rstd_f)

            rstd_unit(0, f_ve, f_rs, ln_f, rstd_f)
            router(0)
            over_units(pool, body)

        @block.vector
        def _(dve):
            v = nc.vector

            for e in range(E):
                last = v.memset(rank[:, :, e:e + 1], float(E - e))
            last.then_inc(consts_made, 1)
            n_split = [0]

            def split(hi, lo, src):
                v.tensor_copy(hi, src).then_inc(split_made, 1)
                n_split[0] += 1
                dve.wait_ge(split_made, n_split[0])
                v.tensor_tensor(lo, src, hi.bitcast(F32), ALU.subtract).then_inc(split_made, 1)
                n_split[0] += 1

            def carry_wait():
                v.memset(spare[:, :], 0.0)

            def ln_stats(src, tiles, st, done, count):
                carry_wait()
                for j in tiles:
                    last = v.bn_stats(st[:, j, :], src(j))
                last.then_inc(done, 1)
                dve.wait_ge(done, count + 1)
                carry_wait()

            def ln_moments(tiles, st, mv, ve, done, count):
                for j in tiles:
                    last = v.bn_aggr(mv[:, j, :], st[:, j, :])
                last.then_inc(done, 1)
                dve.wait_ge(done, count + 2)
                t0, t1 = tiles[0], tiles[-1] + 1
                v.tensor_scalar(ve[:, t0:t1], mv[:, t0:t1, 1:2].rearrange("p a b -> p (a b)"), EPS_LN, None,
                                ALU.add).then_inc(done, 1)

            def ln_apply(src, dst, tiles, mv, rs, done):
                for j in tiles:
                    last = v.tensor_scalar(dst[:, j, :], src(j), mv[:, j, 0:1], rs[:, j:j + 1],
                                           ALU.subtract, ALU.mult)
                last.then_inc(done, 1)

            def pre_norm(k):
                tiles = range(*span(k))
                if isinstance(k, int) and k == 0:
                    dve.wait_ge(ld_x, 16 * NB * TT)
                if parts(k)[1]:
                    wait(dve, mamba_added, k - LAG + 1)
                ln_stats(lambda j: x_tile(k, j), tiles, f_st, ln_f, 4 * k)
                ln_moments(tiles, f_st, f_mv, f_ve, ln_f, 4 * k)

            def pre_apply(k):
                tiles = range(*span(k))
                dve.wait_ge(rstd_f, k + 1)
                wait(dve, x_turned, k)
                ln_apply(lambda j: x_tile(k, j), xn, tiles, f_mv, f_rs, ln_f)

            def pre_split(k):
                t0, t1 = span(k)
                c0, c1 = t0 * P, t1 * P
                dve.wait_ge(x_turned, k + 1)
                wait(dve, work_full, WORK * (k - 1) + E * M)
                v.tensor_copy(x_hi[:, c0:c1], f_bank[:, c0:c1]).then_inc(x_split, 1)
                dve.wait_ge(x_split, 2 * k + 1)
                v.tensor_tensor(x_lo[:, c0:c1], f_bank[:, c0:c1], x_hi[:, c0:c1].bitcast(F32),
                                ALU.subtract).then_inc(x_split, 1)

            def router_a(k):
                t0, t1 = span(k)
                nt = t1 - t0
                base = [ROUTE * k]

                def step(ins):
                    ins.then_inc(route, 1)
                    base[0] = base[0] + 1
                    dve.wait_ge(route, base[0])

                def wide(t):
                    return t[:, t0:t1].rearrange("p (a b) -> p a b", b=1).to_broadcast([P, nt, E])

                bgw = bg_sb[:, :].rearrange("p (a e) -> p a e", a=1).to_broadcast([P, nt, E])
                dve.wait_ge(logits_made, k + 1)
                step(v.tensor_tensor(lg[:, t0:t1], f_bank[:, t0 * E:t1 * E].rearrange("p (a e) -> p a e", e=E),
                                     bgw, ALU.add))
                step(v.tensor_reduce(top[:, t0:t1], lg[:, t0:t1], AX, ALU.max))
                wait(dve, powers, k)
                step(v.tensor_tensor(sh[:, t0:t1], lg[:, t0:t1], wide(top), ALU.subtract))
                step(v.tensor_tensor(eq[:, t0:t1], lg[:, t0:t1], wide(top), ALU.is_equal))
                step(v.tensor_tensor(eq[:, t0:t1], eq[:, t0:t1], rank[:, t0:t1], ALU.mult))
                step(v.tensor_reduce(best[:, t0:t1], eq[:, t0:t1], AX, ALU.max))
                step(v.tensor_tensor(first[:, t0:t1], eq[:, t0:t1], wide(best), ALU.is_equal))
                step(v.scalar_tensor_tensor(lg2[:, t0:t1], first[:, t0:t1], FAR, lg[:, t0:t1], ALU.mult, ALU.add))
                step(v.tensor_reduce(top[:, t0:t1], lg2[:, t0:t1], AX, ALU.max))
                step(v.tensor_tensor(eq[:, t0:t1], lg2[:, t0:t1], wide(top), ALU.is_equal))
                step(v.tensor_tensor(eq[:, t0:t1], eq[:, t0:t1], rank[:, t0:t1], ALU.mult))
                step(v.tensor_reduce(best[:, t0:t1], eq[:, t0:t1], AX, ALU.max))
                step(v.tensor_tensor(both[:, t0:t1], eq[:, t0:t1], wide(best), ALU.is_equal))
                step(v.tensor_tensor(both[:, t0:t1], both[:, t0:t1], first[:, t0:t1], ALU.add))

            def router_b(k):
                t0, t1 = span(k)
                nt = t1 - t0
                base = [ROUTE * k + 14]

                def step(ins):
                    ins.then_inc(route, 1)
                    base[0] = base[0] + 1
                    dve.wait_ge(route, base[0])

                dve.wait_ge(powers, k + 1)
                step(v.tensor_tensor(num[:, t0:t1], ex[:, t0:t1], both[:, t0:t1], ALU.mult))
                step(v.tensor_reduce(whole[:, t0:t1], ex[:, t0:t1], AX, ALU.add))
                step(v.tensor_reduce(den[:, t0:t1], num[:, t0:t1], AX, ALU.add))
                step(v.scalar_tensor_tensor(den[:, t0:t1], whole[:, t0:t1], EPS_GATE, den[:, t0:t1], ALU.mult, ALU.add))
                step(v.reciprocal(den[:, t0:t1], den[:, t0:t1]))
                wait(dve, cw_turned, k)
                wide = den[:, t0:t1].rearrange("p (a b) -> p a b", b=1).to_broadcast([P, nt, E])
                step(v.tensor_tensor(cw[:, t0:t1], num[:, t0:t1], wide, ALU.mult))

            def cw_copy(k):
                t0, t1 = span(k)
                c0, c1 = t0 * P, t1 * P
                dve.wait_ge(cw_turned, k + 1)
                wait(dve, cw_stored, 16 * k)
                wait(dve, out_turned, k)
                v.tensor_copy(cwT[:, c0:c1], f_bank[0:E, c0:c1]).then_inc(cwT_made, 1)

            def gate(k, e):
                t0, t1 = span(k)
                c0, c1 = t0 * P, t1 * P
                dve.wait_ge(work_full, WORK * k + E * M + e + 1)
                if e == 0:
                    dve.wait_ge(cw_spread, 16 * k + 16)
                wait(dve, acc_added, ADDS * k + (max(1, e - 2) if e >= 2 else 0))
                v.tensor_tensor(gated[:, e % 2, c0:c1], work[e % WB][:, c0:c1], cwB[:, e, c0:c1],
                                ALU.mult).then_inc(gate_done, 1)

            def out_norm(k):
                tiles = range(*span(k))
                dve.wait_ge(out_turned, k + 1)
                ln_stats(lambda j: f_bank[:, j * D:(j + 1) * D], tiles, o_st, ln_o, 4 * k)
                ln_moments(tiles, o_st, o_mv, o_ve, ln_o, 4 * k)

            def out_apply(k):
                tiles = range(*span(k))
                dve.wait_ge(rstd_o, k + 1)
                ln_apply(lambda j: f_bank[:, j * D:(j + 1) * D], on, tiles, o_mv, o_rs, ln_o)

            def out_add(k):
                f1, f2 = parts(k)
                dve.wait_ge(affine, 2 * k + 2)
                if f1:
                    v.tensor_tensor(x_chunk(k), x_chunk(k), on[:, 0:TT], ALU.add).then_inc(ffn1_added, 1)
                if f2:
                    v.tensor_tensor(x_chunk(k - LAG), x_chunk(k - LAG), on[:, TT:2 * TT], ALU.add).then_inc(ffn2_added, 1)

            def m_tile(c):
                return lambda j: x_tile(c, j)

            def m_norm(c):
                dve.wait_ge(ffn1_added, c + 1)
                ln_stats(m_tile(c), range(TT), m_st, ln_m, 4 * c)
                ln_moments(range(TT), m_st, m_mv, m_ve, ln_m, 4 * c)

            def m_apply(c):
                dve.wait_ge(rstd_m, c + 1)
                wait(dve, dt_made, c)
                ln_apply(m_tile(c), xm, range(TT), m_mv, m_rs, ln_m)

            def m_split(c):
                dve.wait_ge(xm_turned, c + 1)
                wait(dve, inz_made, c)
                v.tensor_copy(xm_hi[:, :], m_bank[:, 0:CT]).then_inc(xm_split, 1)
                dve.wait_ge(xm_split, 2 * c + 1)
                v.tensor_tensor(xm_lo[:, :], m_bank[:, 0:CT], xm_hi[:, :].bitcast(F32), ALU.subtract).then_inc(xm_split, 1)

            def m_halo(c):
                dve.wait_ge(xpad_made, c + 1)
                v.tensor_copy(xpad[:, :, 0:KC - 1], halo[:, 0]).then_inc(halo_set, 1)
                dve.wait_ge(halo_set, 3 * c + 1)
                v.tensor_copy(halo[:, 0], halo[:, 1]).then_inc(halo_set, 1)
                dve.wait_ge(halo_set, 3 * c + 2)
                v.tensor_copy(halo[:, 1], xpad[:, :, CT:CT + KC - 1]).then_inc(halo_set, 1)

            def m_carry(c):
                dve.wait_ge(carry_kept, NS * c + NS)
                v.tensor_copy(carry[:, 0], carry[:, 1]).then_inc(carry_moved, 1)
                dve.wait_ge(carry_moved, 2 * c + 1)
                v.tensor_copy(carry[:, 1], carry_new[:, :, :]).then_inc(carry_moved, 1)

            def m_conv(c):
                wait(dve, begun, 2 * c)
                for h in range(H):
                    last = v.tensor_scalar(u[:, h], xpad[:, h, 0:CT], convw_sb[:, h, 0:1],
                                           convb_col[:, h:h + 1], ALU.mult, ALU.add)
                last.then_inc(conv, 1)
                for t in range(1, KC):
                    dve.wait_ge(conv, KC * c + t)
                    for h in range(H):
                        last = v.scalar_tensor_tensor(u[:, h], xpad[:, h, t:t + CT], convw_sb[:, h, t:t + 1],
                                                      u[:, h], ALU.mult, ALU.add)
                    last.then_inc(conv, 1)

            def m_silu(c, of_z):
                if of_z:
                    dve.wait_ge(z_read, 2 * c + 2)
                else:
                    dve.wait_ge(x_tanh, c + 1)
                a = flat((zs_next if of_z else u)[:, :, :])
                v.scalar_tensor_tensor(a, flat(tanh), 1.0, a, ALU.add, ALU.mult).then_inc(silu, 1)

            def m_xdbl(c):
                dve.wait_ge(xdbl_made, c + 1)
                wait(dve, dt_made, c)
                v.tensor_copy(dt_low, m_bank[0:R, 0:CT]).then_inc(xdbl_read, 1)
                wait(dve, bc_spread, NS * c)
                v.tensor_copy(bc[0:2 * NS, :], m_bank[R:R + 2 * NS, 0:CT]).then_inc(xdbl_read, 1)
                dve.wait_ge(xdbl_read, 3 * c + 2)
                v.tensor_tensor(bc[2 * NS:4 * NS, :], m_bank[R:R + 2 * NS, 0:CT],
                                bc[0:2 * NS, :].bitcast(F32), ALU.subtract).then_inc(xdbl_read, 1)

            def m_softplus(c):
                base = [SPD * c]

                def step(ins):
                    ins.then_inc(sp_dve, 1)
                    base[0] = base[0] + 1
                    dve.wait_ge(sp_dve, base[0])

                dve.wait_ge(sp_act, 3 * c + 2)
                step(v.scalar_tensor_tensor(flat(sp_s4), flat(sp_tanh), 1.0, flat(sp_exp), ALU.add, ALU.mult))
                dve.wait_ge(sp_act, 3 * c + 3)
                step(v.tensor_scalar(flat(sp_poly), flat(sp_sq), ATANH[4] / 4, None, ALU.mult))
                for co in ATANH[3:0:-1]:
                    step(v.scalar_tensor_tensor(flat(sp_poly), flat(sp_poly), co / 4, flat(sp_sq), ALU.add, ALU.mult))
                step(v.scalar_tensor_tensor(flat(sp_poly), flat(sp_poly), ATANH[0] / 4, flat(sp_s4), ALU.add, ALU.mult))
                dve.wait_ge(dt_read, 2 * c + 2)
                wait(dve, decay_made, NS * c)
                step(v.tensor_tensor(flat(dt[:, :, :]), flat(sp_poly), flat(sp_pos), ALU.add))
                v.tensor_tensor(flat(dtu[:, :, :]), flat(dt[:, :, :]), flat(u[:, :, :]), ALU.mult).then_inc(sp_dve, 1)

            def m_begin(c):
                wait(dve, mamba_made, c)
                for h in range(H):
                    last = v.tensor_scalar(y_acc[:, h], u[:, h], dpar_col[:, h:h + 1], None, ALU.mult)
                last.then_inc(begun, 1)
                v.tensor_copy(flat(zs[:, :, :]), flat(zs_next[:, :, :])).then_inc(begun, 1)

            def m_state(c, n):
                def wide(m, half):
                    return bc_bank[m % BB][:, half * CT:(half + 1) * CT].rearrange(
                        "p (a t) -> p a t", a=1).to_broadcast([P, H, CT])

                if n < NS:
                    dve.wait_ge(bc_spread, NS * c + n + 1)
                    if n == 0:
                        dve.wait_ge(sp_dve, SPD * c + SPD)
                    if n >= 2:
                        dve.wait_ge(scanned, NS * c + n - 1)
                    v.tensor_tensor(drive[:, n % 2], dtu[:, :, :], wide(n, 0), ALU.mult).then_inc(drive_made, 1)
                if n >= 1:
                    dve.wait_ge(scanned, NS * c + n)
                    wait(dve, y_added, NS * c + n - 2)
                    v.tensor_tensor(seen[:, (n - 1) % 2], state[:, (n - 1) % 2], wide(n - 1, 1),
                                    ALU.mult).then_inc(seen_made, 1)
                if n < NS:
                    dve.wait_ge(drive_made, NS * c + n + 1)
                    dve.wait_ge(decay_made, NS * c + n + 1)
                    wait(dve, carry_kept, NS * c + n - 1)
                    if n >= 2:
                        dve.wait_ge(seen_made, NS * c + n - 1)
                    if n == 0:
                        wait(dve, carry_moved, 2 * c)
                    for h in range(H):
                        last = v.tensor_tensor_scan(state[:, n % 2, h], decay[:, n % NSLOT, h], drive[:, n % 2, h],
                                                    carry[:, 0, h, n:n + 1], ALU.mult, ALU.add)
                    last.then_inc(scanned, 1)

            def m_gate(c):
                dve.wait_ge(y_added, NS * c + NS)
                dve.wait_ge(begun, 2 * c + 2)
                v.tensor_tensor(flat(y_acc[:, :, :]), flat(y_acc[:, :, :]), flat(zs[:, :, :]), ALU.mult).then_inc(y_gated, 1)

            def m_add(c):
                dve.wait_ge(mamba_made, c + 1)
                v.tensor_tensor(x_chunk(c), x_chunk(c), m_bank[:, 0:TT * D].rearrange("p (a d) -> p a d", d=D),
                                ALU.add).then_inc(mamba_added, 1)

            dve.wait_ge(ld_vec, 16 * 6)
            split(wg_hi[:, :], wg_lo[:, :], hid[:, E, 0:E])
            pre_norm(0)
            dve.wait_ge(consts_made, 1)
            dve.wait_ge(pool_setup, 2)
            pre_apply(0)
            for e in range(2):
                dve.wait_ge(ld_w1[e], 16)
                split(w1_hi[:, e], w1_lo[:, e], hid[:, e, :])
            pre_split(0)
            router_a(0)
            for e in range(2, E):
                dve.wait_ge(ld_w1[e], 16)
                split(w1_hi[:, e], w1_lo[:, e], hid[:, e, :])
            dve.wait_ge(ld_mamba, 16 * 8)
            split(win_hi[:, :], win_lo[:, :], hid[:, E + 1, 0:2 * DI])
            dve.wait_ge(cols_turned, 1)
            v.tensor_copy(cols[:, :], m_bank[:, 0:ROWS]).then_inc(cols_made, 1)
            dve.wait_ge(cols_made, 1)
            v.tensor_scalar(convb_col, convb_col, 0.5, None, ALU.mult)
            v.tensor_scalar(flat(convw_sb[:, :, :]), flat(convw_sb[:, :, :]), 0.5, None, ALU.mult)
            v.tensor_scalar(gamma_h[:, :], gamma_h[:, :], 0.5, None, ALU.mult).then_inc(scaled, 1)
            v.tensor_scalar(beta_h[:, :], beta_h[:, :], 0.5, None, ALU.mult).then_inc(scaled, 1)
            dve.wait_ge(ident_made, 1)
            v.tensor_copy(pick[0:2 * NS, :], ident[0:2 * NS, 0:2 * NS])
            v.tensor_copy(pick[2 * NS:4 * NS, :], ident[2 * NS:4 * NS, 2 * NS:4 * NS]).then_inc(cols_made, 1)
            dve.wait_ge(a_exp, 1)
            v.tensor_scalar(flat(a_neg[:, :, :]), flat(a_neg[:, :, :]), -1.0, None, ALU.mult).then_inc(cols_made, 1)
            def body(k):
                c1, c2, c3 = k - 1, k - 2, k - 3
                for e in range(E):
                    if e == 0 and unit_ok(k) and not (isinstance(k, int) and k == 0):
                        router_a(k)
                    if chunk_ok(c3):
                        m_state(c3, N_A + e)
                    if chunk_ok(c2):
                        if e == 0:
                            m_halo(c2)
                        if e == 1:
                            m_conv(c2)
                        if e == 2:
                            m_silu(c2, True)
                        if e == 4:
                            m_silu(c2, False)
                        if e == 5:
                            m_xdbl(c2)
                    if unit_ok(k - 1):
                        if e == 2:
                            out_norm(k - 1)
                        if e == 3:
                            out_apply(k - 1)
                        if e == 4:
                            out_add(k - 1)
                    if e == 2 and unit_ok(k):
                        router_b(k)
                    if chunk_ok(c1):
                        if e == 4:
                            m_norm(c1)
                        if e == 6:
                            m_apply(c1)
                    if e == 5 and unit_ok(k):
                        cw_copy(k)
                if chunk_ok(c3):
                    m_carry(c3)
                for e in range(E):
                    if unit_ok(k):
                        gate(k, e)
                    if e == 0 and chunk_ok(c3):
                        m_gate(c3)
                    if e == 1 and chunk_ok(c2):
                        m_softplus(c2)
                    if e == 2:
                        if chunk_ok(c3):
                            m_add(c3)
                        if chunk_ok(c2):
                            m_begin(c2)
                    if e == 4 and chunk_ok(c1):
                        m_split(c1)
                    if unit_ok(k + 1):
                        if e == 3:
                            pre_norm(k + 1)
                        if e == 4:
                            pre_apply(k + 1)
                        if e == 6:
                            pre_split(k + 1)
                    if chunk_ok(c2):
                        for n in N_OF[e]:
                            m_state(c2, n)

            over_units(dve, body)

        @block.scalar
        def _(act):
            s = nc.scalar
            act.dma_start(gamma_h[:, :], gamma.rearrange("(a e) -> a e", a=1).to_broadcast([P, D])).then_inc(ld_mamba, 16)
            act.dma_start(beta_h[:, :], beta.rearrange("(a e) -> a e", a=1).to_broadcast([P, D])).then_inc(ld_mamba, 16)
            act.dma_start(a_neg[:, :, :], a_log.rearrange("(h p) n -> p h n", p=P)).then_inc(ld_mamba, 16)
            act.dma_start(convw_sb[:, :, :], conv_w.rearrange("(h p) n -> p h n", p=P)).then_inc(ld_mamba, 16)
            act.dma_start(b2_sb[:, :], b2).then_inc(ld_w2, 16)
            for e in range(E):
                act.dma_start(w2[:, e], W2[e].rearrange("(m p) d -> p m d", p=P)).then_inc(ld_w2, 16)
            act.wait_ge(ld_mamba, 16 * 8)
            s.activation(flat(a_neg[:, :, :]), flat(a_neg[:, :, :]), ACT.Exp).then_inc(a_exp, 1)
            act.wait_ge(cols_made, 1)

            def gelu(k, e, m):
                t0, t1 = span(k)
                c0, c1 = t0 * P, t1 * P
                i = e * M + m
                act.wait_ge(work_full, WORK * k + i + 1)
                if isinstance(k, int) and k == 0 and i == 0:
                    act.wait_ge(split_made, 2 * (E + 2))
                s.activation(hid[:, i, c0:c1], work[i % WB][:, c0:c1], ACT.Gelu,
                             bias=b1_col[:, i:i + 1]).then_inc(gelu_done, 1)

            def m_xin(c):
                act.wait_ge(inx_made, c + 1)
                wait(act, conv, KC * c)
                wait(act, halo_set, 3 * c)
                s.activation(xpad[:, :, KC - 1:], m_bank[:, :].rearrange("p (h t) -> p h t", h=H),
                             ACT.Copy).then_inc(xpad_made, 1)

            def m_zin(c):
                act.wait_ge(inz_made, c + 1)
                wait(act, begun, 2 * c)
                s.activation(flat(zs_next[:, :, :]), m_bank[:, :], ACT.Copy, scale=0.5).then_inc(z_read, 1)
                wait(act, acc_added, ADDS * (c + 2))
                s.activation(flat(tanh), m_bank[:, :], ACT.Tanh, scale=0.5).then_inc(z_read, 1)

            def m_xtanh(c):
                act.wait_ge(conv, KC * c + KC)
                act.wait_ge(silu, 2 * c + 1)
                s.activation(flat(tanh), flat(u[:, :, :]), ACT.Tanh).then_inc(x_tanh, 1)

            def m_softplus(c):
                act.wait_ge(dt_made, c + 1)
                if isinstance(c, int) and c == 0:
                    act.wait_ge(pool_setup, 2)
                wait(act, scanned, NS * c)
                wait(act, seen_made, NS * c)
                wait(act, carry_kept, NS * c)
                for h in range(H):
                    src = m_bank[:, h * CT:(h + 1) * CT]
                    last = s.activation(sp_abs[:, h], src, ACT.Abs, bias=dtb_col[:, h:h + 1])
                last.then_inc(dt_read, 1)
                for h in range(H):
                    src = m_bank[:, h * CT:(h + 1) * CT]
                    last = s.activation(sp_pos[:, h], src, ACT.Relu, bias=dtb_col[:, h:h + 1])
                last.then_inc(dt_read, 1)
                act.wait_ge(dt_read, 2 * c + 1)
                s.activation(flat(sp_exp), flat(sp_abs), ACT.Exp, scale=-1.0).then_inc(sp_act, 1)
                s.activation(flat(sp_tanh), flat(sp_abs), ACT.Tanh, scale=0.5, bias=half_ln2[:, :]).then_inc(sp_act, 1)
                act.wait_ge(sp_dve, SPD * c + 1)
                s.activation(flat(sp_sq), flat(sp_s4), ACT.Square, scale=0.25).then_inc(sp_act, 1)

            def decays(c, n):
                if n == 0:
                    act.wait_ge(sp_dve, SPD * c + SPD - 1)
                wait(act, scanned, NS * c + n - NSLOT + 1)
                for h in range(H):
                    last = s.activation(decay[:, n % NSLOT, h], dt[:, h], ACT.Exp, scale=a_neg[:, h, n:n + 1])
                last.then_inc(decay_made, 1)

            def body(k):
                c1, c2 = k - 1, k - 2
                for e in range(E):
                    if unit_ok(k):
                        for m in range(M):
                            gelu(k, e, m)
                    if chunk_ok(c2):
                        if e == 1:
                            m_zin(c2)
                        if e == 3:
                            m_xtanh(c2)
                if chunk_ok(c2):
                    m_softplus(c2)
                    for n in range(NS):
                        decays(c2, n)
                if chunk_ok(c1):
                    m_xin(c1)

            over_units(act, body)

        @block.tensor
        def _(pe):
            t = nc.tensor

            def three(dst, hi_w, lo_w, hi_x, lo_x):
                t.matmul(dst, hi_w, hi_x, start=True, stop=False)
                t.matmul(dst, hi_w, lo_x, start=False, stop=False)
                return t.matmul(dst, lo_w, hi_x, start=False, stop=True)

            def last_use(uses, i):
                return max(j for j in range(uses) if j % WB == i)

            def turn_x(k):
                pe.wait_ge(ln_f, 4 * k + 4)
                wait(pe, cwT_made, k)
                for j in range(*span(k)):
                    last = t.transpose(f_bank[:, j * P:(j + 1) * P], xn[:, j, :], ident[:, :])
                last.then_inc(x_turned, 1)

            def logits(k):
                pe.wait_ge(x_split, 2 * k + 2)
                for j in range(*span(k)):
                    xh, xl = x_hi[:, j * P:(j + 1) * P], x_lo[:, j * P:(j + 1) * P]
                    dst = f_bank[:, j * E:(j + 1) * E]
                    t.matmul(dst, xh, wg_hi[:, :], start=True, stop=False)
                    t.matmul(dst, xh, wg_lo[:, :], start=False, stop=False)
                    last = t.matmul(dst, xl, wg_hi[:, :], start=False, stop=True)
                last.then_inc(logits_made, 1)

            def turn_cw(k):
                pe.wait_ge(route, ROUTE * k + ROUTE)
                wait(pe, ln_o, 4 * k)
                for j in range(*span(k)):
                    last = t.transpose(f_bank[0:E, j * P:(j + 1) * P], cw[:, j, :], ident[:, :])
                last.then_inc(cw_turned, 1)

            def w1(k, e, m):
                t0, t1 = span(k)
                c0, c1 = t0 * P, t1 * P
                i = e * M + m
                if isinstance(k, int) and k == 0 and m == 0:
                    pe.wait_ge(split_made, 2 * (e + 2))
                if i < WB:
                    wait(pe, gate_done, E * (k - 1) + last_use(E, i) + 1)
                else:
                    pe.wait_ge(gelu_done, E * M * k + i - WB + 1)
                cut = slice(m * P, (m + 1) * P)
                three(work[i % WB][:, c0:c1], w1_hi[:, e, cut], w1_lo[:, e, cut],
                      x_hi[:, c0:c1], x_lo[:, c0:c1]).then_inc(work_full, 1)

            def w2_(k, e):
                t0, t1 = span(k)
                c0, c1 = t0 * P, t1 * P
                if e < WB:
                    pe.wait_ge(gelu_done, E * M * k + last_use(E * M, e) + 1)
                else:
                    pe.wait_ge(gate_done, E * k + e - WB + 1)
                if isinstance(k, int) and k == 0 and e == 0:
                    pe.wait_ge(ld_w2, 16 * (E + 1))
                for m in range(M):
                    last = t.matmul(work[e % WB][:, c0:c1], w2[:, e, m, :], hid[:, e * M + m, c0:c1],
                                    start=m == 0, stop=m == M - 1)
                last.then_inc(work_full, 1)

            def turn_out(k):
                pe.wait_ge(acc_added, ADDS * k + ADDS)
                if unit_ok(k + 1):
                    pe.wait_ge(route, ROUTE * (k + 1) + 1)
                for j in range(*span(k)):
                    dst = f_bank[:, j * D:(j + 1) * D]
                    t.matmul(dst, acc[:, j * P:(j + 1) * P], ident[:, :], start=True, stop=False)
                    last = t.matmul(dst, cwT[:, j * P:(j + 1) * P], b2_sb[:, :], start=False, stop=True)
                last.then_inc(out_turned, 1)

            def turn_xm(c):
                pe.wait_ge(ln_m, 4 * c + 4)
                wait(pe, mamba_added, c - 1)
                for j in range(TT):
                    last = t.transpose(m_bank[:, j * P:(j + 1) * P], xm[:, j, :], ident[:, :])
                last.then_inc(xm_turned, 1)

            def in_proj(c, z, done):
                pe.wait_ge(xm_split, 2 * c + 2)
                if z:
                    pe.wait_ge(xpad_made, c + 1)
                for h in range(H):
                    at = z * DI + h * P
                    last = three(m_bank[:, h * CT:(h + 1) * CT], win_hi[:, at:at + P], win_lo[:, at:at + P],
                                 xm_hi[:, :], xm_lo[:, :])
                last.then_inc(done, 1)

            def x_proj(c):
                pe.wait_ge(silu, 2 * c + 2)
                pe.wait_ge(z_read, 2 * c + 2)
                for h in range(H):
                    last = t.matmul(m_bank[0:R + 2 * NS, 0:CT], xp_sb[:, h, :], u[:, h, :], start=h == 0, stop=h == H - 1)
                last.then_inc(xdbl_made, 1)

            def dt_proj(c):
                pe.wait_ge(xdbl_read, 3 * c + 3)
                for h in range(H):
                    last = t.matmul(m_bank[:, h * CT:(h + 1) * CT], dtw_sb[:, h * P:(h + 1) * P], dt_low,
                                    start=True, stop=True)
                last.then_inc(dt_made, 1)

            def spread(c, n):
                pe.wait_ge(xdbl_read, 3 * c + 3)
                wait(pe, seen_made, NS * c + max(n - BB + 1, 0))
                bank = bc_bank[n % BB]
                for i, row in enumerate((n, NS + n)):
                    one = pick[:, row:row + 1].to_broadcast([4 * NS, P])
                    last = t.matmul(bank[:, i * CT:(i + 1) * CT], one, bc[:, :], start=True, stop=True)
                last.then_inc(bc_spread, 1)

            def out_proj(c):
                pe.wait_ge(y_gated, c + 1)
                if chunk_ok(c + 1):
                    pe.wait_ge(dt_read, 2 * (c + 1) + 2)
                for j in range(TT):
                    for h in range(H):
                        last = t.matmul(m_bank[:, j * D:(j + 1) * D], y_acc[:, h, j * P:(j + 1) * P], wout_sb[:, h, :],
                                        start=h == 0, stop=h == H - 1)
                last.then_inc(mamba_made, 1)

            pe.wait_ge(ident_made, 1)
            pe.wait_ge(ld_vec, 16 * 6)
            t.transpose(m_bank[:, 0:ROWS], rows, ident[0:ROWS, 0:ROWS]).then_inc(cols_turned, 1)
            turn_x(0)
            logits(0)

            def body(k):
                c1, c2, c3 = k - 1, k - 2, k - 3
                for e in range(E):
                    if unit_ok(k):
                        for m in range(M):
                            w1(k, e, m)
                    if chunk_ok(c3) and N_A + e < NS:
                        spread(c3, N_A + e)
                    if e == 2 and unit_ok(k - 1):
                        turn_out(k - 1)
                    if e == 5 and unit_ok(k):
                        turn_cw(k)
                    if not chunk_ok(c2):
                        continue
                    if e == 1:
                        in_proj(c2, 1, inz_made)
                    if e == 5:
                        x_proj(c2)
                    if e == 7:
                        dt_proj(c2)
                for e in range(E):
                    if unit_ok(k):
                        w2_(k, e)
                    if e == 2 and chunk_ok(c3):
                        out_proj(c3)
                    if chunk_ok(c2):
                        if e == 1:
                            pe.wait_ge(cols_made, 2)
                        for n in N_OF[e]:
                            spread(c2, n)
                    if chunk_ok(c1):
                        if e == 4:
                            turn_xm(c1)
                        if e == 6:
                            in_proj(c1, 0, inx_made)
                    if e == 5 and unit_ok(k + 1):
                        turn_x(k + 1)
                    if e == 7 and unit_ok(k + 1):
                        logits(k + 1)

            over_units(pe, body)


_INS = ["L0_attn_hidden_states", "L0_attn_in_proj_w", "L0_attn_conv_w", "L0_attn_conv_b", "L0_attn_x_proj_w",
        "L0_attn_dt_proj_w", "L0_attn_dt_bias", "L0_attn_A_log", "L0_attn_D_param", "L0_attn_out_proj_w",
        "L0_ffn_Wg", "L0_ffn_bg", "L0_ffn_W1", "L0_ffn_b1", "L0_ffn_W2", "L0_ffn_b2", "L0_ffn_gamma", "L0_ffn_beta"]


def kernel(**inputs):
    import numpy as np
    import concourse.bacc as bacc
    from concourse.bass_utils import run_bass_kernel_spmd

    nc = bacc.Bacc("TRN2", target_bir_lowering=False, num_devices=1)
    arrays, args = {}, []
    for name in _INS:
        a = np.ascontiguousarray(inputs[name])
        arrays[f"in_{name}"] = a
        args.append(nc.dram_tensor(f"in_{name}", a.shape, mybir.dt.from_np(a.dtype), kind="ExternalInput").ap())
    experts = arrays["in_L0_ffn_W1"].shape[0]
    args.append(nc.dram_tensor("gate_scratch", (experts, 2 * CT), F32, kind="Internal").ap())
    shape = arrays["in_L0_attn_hidden_states"].shape
    args.append(nc.dram_tensor("out", shape, F32, kind="ExternalOutput").ap())
    macaron(nc, *args)
    return run_bass_kernel_spmd(nc, [arrays], core_ids=[0]).results[0]["out"]
```

```python
from contextlib import ExitStack

import concourse.bass as bass
from concourse import mybir

F32 = mybir.dt.float32
F32R = mybir.dt.float32r
ALU = mybir.AluOpType
ACT = mybir.ActivationFunctionType
AX = mybir.AxisListType.X

P = 128
CT = 256
TT = CT // P
LAG = 4
EPS_LN = 1e-5
EPS_GATE = 1e-8
FAR = -3.0e38
NSLOT = 8
WB = 3
SPREAD = 2
BB = 3
HALF_LN2 = 0.34657359027997264
LEAD = 0.28174657258139
A1, A0 = 1.267423698171514, 1.1272198435930603
B1, B0 = -0.7712079220645582, 2.0020421682902847


def wait(eng, sem, value):
    if isinstance(value, int) and value <= 0:
        return
    eng.wait_ge(sem, value)


def macaron(nc, hidden, in_w, conv_w, conv_b, xp_w, dt_w, dt_b, a_log, d_par, out_w,
            Wg, bg, W1, b1, W2, b2, gamma, beta, cw_dram, out):
    NB, L, D = hidden.shape
    E, _, DFF = W1.shape
    M = DFF // P
    DI = in_w.shape[1] // 2
    H = DI // P
    NS = a_log.shape[1]
    KC = conv_w.shape[1]
    R = dt_w.shape[0]
    CHUNKS = NB * L // CT
    NT = CHUNKS * TT
    UNITS = CHUNKS + LAG
    LOOP = (LAG + 1, CHUNKS - 1)
    WORK = E * M + E
    ADDS = E - 1
    NB1 = E * M
    ROWS = NB1 + 3 * H

    with ExitStack() as ctx:
        def sb(name, shape, dt=F32):
            return ctx.enter_context(nc.sbuf_tensor(name, shape, dt))

        def sem(name):
            return ctx.enter_context(nc.semaphore(name))

        def flat(ap):
            return ap.rearrange("p a b -> p (a b)")

        w1_hi = sb("w1_hi", [P, E, DFF], F32R)
        w1_lo = sb("w1_lo", [P, E, DFF], F32R)
        w2 = sb("w2", [P, E, M, D])
        wg_hi = sb("wg_hi", [P, E], F32R)
        wg_lo = sb("wg_lo", [P, E], F32R)
        win_hi = sb("win_hi", [P, 2 * DI], F32R)
        win_lo = sb("win_lo", [P, 2 * DI], F32R)
        xp_sb = sb("xp_sb", [P, H, R + 2 * NS])
        dtw_sb = sb("dtw_sb", [R, DI])
        wout_sb = sb("wout_sb", [P, H, D])
        b2_sb = sb("b2_sb", [E, D])
        gamma_h = sb("gamma_h", [P, D])
        beta_h = sb("beta_h", [P, D])
        bg_sb = sb("bg_sb", [P, E])
        cols = sb("cols", [P, ROWS])
        convw_sb = sb("convw_sb", [P, H, KC])
        a_neg = sb("a_neg", [P, H, NS])
        ident = sb("ident", [P, P])
        pick = sb("pick", [2 * 2 * NS, 2 * NS], F32R)
        mhalf = sb("mhalf", [P, 2 * TT])
        rank = sb("rank", [P, 2 * TT, E])
        b1_col = cols[:, 0:NB1]
        convb_col = cols[:, NB1:NB1 + H]
        dtb_col = cols[:, NB1 + H:NB1 + 2 * H]
        dpar_col = cols[:, NB1 + 2 * H:ROWS]

        xs = sb("xs", [P, NT, D])
        hid = sb("hid", [P, E * M, 2 * CT])
        rows = hid[0:ROWS, E + 2, 0:P]
        cwB = sb("cwB", [P, E, 2 * CT])
        cwT = sb("cwT", [E, 2 * CT])
        xn = sb("xn", [P, 2 * TT, D])
        x_hi = sb("x_hi", [P, 2 * CT], F32R)
        x_lo = sb("x_lo", [P, 2 * CT], F32R)
        gated = sb("gated", [P, 2, 2 * CT])
        acc = sb("acc", [P, 2 * CT])
        on = xn
        f_st = sb("f_st", [P, 2 * TT, 6])
        f_mv = sb("f_mv", [P, 2 * TT, 2])
        f_ve = sb("f_ve", [P, 2 * TT])
        f_rs = sb("f_rs", [P, 2 * TT])
        o_st = sb("o_st", [P, 2 * TT, 6])
        o_mv = sb("o_mv", [P, 2 * TT, 2])
        o_ve = sb("o_ve", [P, 2 * TT])
        o_rs = sb("o_rs", [P, 2 * TT])
        lg = sb("lg", [P, 2 * TT, E])
        lg2 = sb("lg2", [P, 2 * TT, E])
        sh = sb("sh", [P, 2 * TT, E])
        ex = sb("ex", [P, 2 * TT, E])
        num = lg2
        cw = sb("cw", [P, 2 * TT, E])
        eq = sb("eq", [P, 2 * TT, E])
        first = sb("first", [P, 2 * TT, E])
        both = sb("both", [P, 2 * TT, E])
        top = sb("top", [P, 2 * TT])
        best = sb("best", [P, 2 * TT])
        whole = sb("whole", [P, 2 * TT])
        den = sb("den", [P, 2 * TT])
        spare = sb("spare", [P, 1])
        sp_bias = sb("sp_bias", [P, 3])

        xm = sb("xm", [P, TT, D])
        xm_hi = sb("xm_hi", [P, CT], F32R)
        xm_lo = sb("xm_lo", [P, CT], F32R)
        m_st = sb("m_st", [P, TT, 6])
        m_mv = sb("m_mv", [P, TT, 2])
        m_ve = sb("m_ve", [P, TT])
        m_rs = sb("m_rs", [P, TT])
        xpad = sb("xpad", [P, H, KC - 1 + CT])
        halo = sb("halo", [P, 2, H, KC - 1])
        u = sb("u", [P, H, CT])
        zs_next = sb("zs_next", [P, H, CT])
        z_tanh, x_tanh = gated[:, 0], gated[:, 1]
        zs = sb("zs", [P, H, CT])
        dt_low = flat(xm[:, :, :])[0:R]
        bc = sb("bc", [4 * NS, CT], F32R)
        dt = sb("dt", [P, H, CT])
        dtu = sb("dtu", [P, H, CT])
        decay = sb("decay", [P, NSLOT, H, CT])
        drive = sb("drive", [P, 2, H, CT])
        state = sb("state", [P, 2, H, CT])
        seen = sb("seen", [P, 2, H, CT])
        y_acc = sb("y_acc", [P, H, CT])
        carry = sb("carry", [P, 2, H, NS])
        carry_new = sb("carry_new", [P, H, NS])

        sp_abs, sp_exp = drive[:, 0], xn[:, :, :].rearrange("p (h r) d -> p h (r d)", h=H)
        sp_pos, sp_tanh, sp_b = dt[:, :, :], sp_abs, sp_abs
        sp_s4, sp_sq, sp_a = sp_exp, drive[:, 1], drive[:, 1]

        work = [ctx.enter_context(nc.psum_tensor(f"work{i}", [P, 512], F32)) for i in range(WB)]
        f_bank = ctx.enter_context(nc.psum_tensor("f_bank", [P, 512], F32))
        m_bank = ctx.enter_context(nc.psum_tensor("m_bank", [P, 512], F32))
        bc_bank = [ctx.enter_context(nc.psum_tensor(f"bc_bank{i}", [P, 512], F32)) for i in range(BB)]

        ld_x = sem("ld_x")
        ld_w1 = [sem(f"ld_w1_{e}") for e in range(E)]
        ld_w2 = sem("ld_w2")
        ld_vec = sem("ld_vec")
        ld_mamba = sem("ld_mamba")
        consts_made = sem("consts_made")
        ident_made = sem("ident_made")
        pool_setup = sem("pool_setup")
        split_made = sem("split_made")
        cols_turned = sem("cols_turned")
        cols_made = sem("cols_made")
        a_exp = sem("a_exp")
        scaled = sem("scaled")
        ln_f = sem("ln_f")
        rstd_f = sem("rstd_f")
        x_turned = sem("x_turned")
        x_split = sem("x_split")
        logits_made = sem("logits_made")
        route = sem("route")
        tanhs = sem("tanhs")
        cw_turned = sem("cw_turned")
        cwT_made = sem("cwT_made")
        cw_stored = sem("cw_stored")
        cw_spread = [sem(f"cw_spread_{i}") for i in range(E // SPREAD)]
        work_full = sem("work_full")
        gelu_done = sem("gelu_done")
        gate_done = sem("gate_done")
        acc_added = sem("acc_added")
        out_turned = sem("out_turned")
        ln_o = sem("ln_o")
        rstd_o = sem("rstd_o")
        affine = sem("affine")
        ffn1_added = sem("ffn1_added")
        ffn2_added = sem("ffn2_added")
        stored = sem("stored")
        ln_m = sem("ln_m")
        rstd_m = sem("rstd_m")
        xm_turned = sem("xm_turned")
        xm_split = sem("xm_split")
        inx_made = sem("inx_made")
        inz_made = sem("inz_made")
        xpad_made = sem("xpad_made")
        halo_set = sem("halo_set")
        z_read = sem("z_read")
        conv = sem("conv")
        x_tanhed = sem("x_tanhed")
        silu = sem("silu")
        xdbl_made = sem("xdbl_made")
        xdbl_read = sem("xdbl_read")
        dt_made = sem("dt_made")
        dt_read = sem("dt_read")
        sp_act = sem("sp_act")
        sp_dve = sem("sp_dve")
        begun = sem("begun")
        bc_spread = sem("bc_spread")
        decay_made = sem("decay_made")
        drive_made = sem("drive_made")
        scanned = sem("scanned")
        seen_made = sem("seen_made")
        y_added = sem("y_added")
        carry_kept = sem("carry_kept")
        carry_moved = sem("carry_moved")
        y_gated = sem("y_gated")
        mamba_made = sem("mamba_made")
        mamba_added = sem("mamba_added")

        N_OF = {0: [], 1: [], 2: [0], 3: [1, 2], 4: [3, 4], 5: [5, 6], 6: [7], 7: [8]}
        N_A = 9
        N_HIGH, N_X, N_XIN = 11, 13, 14
        ROUTE = 23
        ROUTES = {0: range(10), 1: range(10, 14), 2: range(14, 19), 3: range(19, ROUTE)}
        ROUTES.update({e: () for e in range(4, E)})
        SPD = 6
        SPA = 5

        def parts(k):
            if not isinstance(k, int):
                return True, True
            return 0 <= k < CHUNKS, LAG <= k < UNITS

        def span(k):
            f1, f2 = parts(k)
            return (0 if f1 else TT), (2 * TT if f2 else TT)

        def chunk_ok(c):
            return not isinstance(c, int) or 0 <= c < CHUNKS

        def unit_ok(k):
            return not isinstance(k, int) or 0 <= k < UNITS

        def x_tile(k, j):
            at = TT * k + j if j < TT else TT * (k - LAG) + j - TT
            return xs[:, at, :] if isinstance(at, int) else xs[:, bass.ds(at, 1), :].rearrange("p a d -> p (a d)")

        def x_chunk(c):
            at = TT * c
            return xs[:, at:at + TT, :] if isinstance(at, int) else xs[:, bass.ds(at, TT), :]

        def over_units(eng, body):
            for k in range(LOOP[0]):
                body(k)
            with eng.Fori(*LOOP) as k:
                body(k)
            for k in range(LOOP[1], UNITS + 1):
                body(k)

        def bc_wide(n, half):
            return bc_bank[n % BB][:, half * CT:(half + 1) * CT].rearrange(
                "p (a t) -> p a t", a=1).to_broadcast([P, H, CT])

        block = ctx.enter_context(nc.Block())

        @block.sync
        def _(sp):
            for b in range(NB):
                for r in range(TT):
                    dst = xs[:, :, :].rearrange("p (q b r) d -> p q b r d", b=NB, r=TT)[:, :, b, r]
                    src = hidden[b].rearrange("(q r p) d -> p q r d", p=P, r=TT)[:, :, r]
                    sp.dma_start(dst, src).then_inc(ld_x, 16)
            sp.dma_start(rows[0:NB1, :], b1.rearrange("e (m p) -> (e m) p", p=P)).then_inc(ld_vec, 16)
            for i, v in enumerate((conv_b, dt_b, d_par)):
                sp.dma_start(rows[NB1 + H * i:NB1 + H * i + H, :],
                             v.rearrange("(h p) -> h p", p=P)).then_inc(ld_vec, 16)
            sp.dma_start(bg_sb[:, :], bg.rearrange("(a e) -> a e", a=1).to_broadcast([P, E])).then_inc(ld_vec, 16)
            sp.dma_start(hid[:, E, 0:E], Wg).then_inc(ld_vec, 16)
            for e in range(E):
                sp.dma_start(hid[:, e, :], W1[e]).then_inc(ld_w1[e], 16)
            sp.dma_start(hid[:, E + 1, 0:2 * DI], in_w).then_inc(ld_mamba, 16)
            sp.dma_start(xp_sb[:, :, :], xp_w.rearrange("(h p) n -> p h n", p=P)).then_inc(ld_mamba, 16)
            sp.dma_start(dtw_sb[:, :], dt_w).then_inc(ld_mamba, 16)
            sp.dma_start(wout_sb[:, :, :], out_w.rearrange("(h p) n -> p h n", p=P)).then_inc(ld_mamba, 16)

            def gates(k):
                t0, t1 = span(k)
                c0, c1 = t0 * P, t1 * P
                wait(sp, cwT_made, k + 1)
                sp.dma_start(cw_dram[:, c0:c1], cwT[:, c0:c1]).then_inc(cw_stored, 16)
                wait(sp, gate_done, E * k)
                sp.wait_ge(cw_stored, 16 * k + 16)
                for i in range(E // SPREAD):
                    e0, e1 = SPREAD * i, SPREAD * i + SPREAD
                    src = cw_dram[e0:e1, c0:c1].rearrange("(a e) c -> a e c", a=1).to_broadcast([P, SPREAD, c1 - c0])
                    sp.dma_start(cwB[:, e0:e1, c0:c1], src).then_inc(cw_spread[i], 16)

            def store(q, b):
                rows_out = out[b].rearrange("(q p) d -> p q d", p=P)
                if isinstance(q, int):
                    c = NB * q + b
                    dst, src = rows_out[:, TT * q:TT * q + TT, :], xs[:, TT * c:TT * c + TT, :]
                else:
                    to = sp.snap(TT * q)
                    at = sp.snap(TT * NB * q + TT * b)
                    dst, src = rows_out[:, bass.ds(to, TT), :], xs[:, bass.ds(at, TT), :]
                sp.wait_ge(ffn2_added, NB * q + b + 1)
                sp.dma_start(dst, src).then_inc(stored, 16)

            for k in range(LAG + 1):
                gates(k)
            with sp.Fori(0, (CHUNKS - LAG - 1) // NB) as q:
                for b in range(NB):
                    gates(NB * q + LAG + 1 + b)
                    store(q, b)
            for c in range((CHUNKS - LAG - 1) // NB * NB, CHUNKS):
                if c + LAG + 1 < UNITS:
                    gates(c + LAG + 1)
                store(c // NB, c % NB)
            sp.wait_ge(stored, 16 * CHUNKS)

        @block.gpsimd
        def _(pool):
            g = nc.gpsimd
            g.memset(ident[:, :], 0.0).then_inc(pool_setup, 1)
            pool.wait_ge(pool_setup, 1)
            g.affine_select(out=ident[:, :], in_=ident[:, :], compare_op=ALU.not_equal, fill=1.0, base=0,
                            pattern=[[-1, P]], channel_multiplier=1).then_inc(ident_made, 1)
            g.memset(mhalf[:, :], -0.5)
            for i, value in enumerate((HALF_LN2, A1, B1)):
                g.memset(sp_bias[:, i:i + 1], value)
            g.memset(halo[:, :, :, :], 0.0)
            g.memset(carry[:, :, :, :], 0.0).then_inc(pool_setup, 1)
            pool.wait_ge(pool_setup, 2)

            def rstd_unit(k, ve, rs, needed, done):
                t0, t1 = span(k)
                pool.wait_ge(needed, 4 * k + 3)
                g.tensor_tensor(rs[:, t0:t1], ve[:, t0:t1], mhalf[:, t0:t1], ALU.pow).then_inc(done, 1)

            def add_state(c, n):
                pool.wait_ge(seen_made, NS * c + n + 1)
                if n == 0:
                    wait(pool, carry_moved, 2 * c)
                    pool.wait_ge(begun, 2 * c + 1)
                else:
                    pool.wait_ge(y_added, NS * c + n)
                g.tensor_tensor(flat(y_acc[:, :, :]), flat(y_acc[:, :, :]), flat(seen[:, n % 2]),
                                ALU.add).then_inc(y_added, 1)
                g.tensor_copy(carry_new[:, :, n:n + 1], state[:, n % 2, :, CT - 1:CT]).then_inc(carry_kept, 1)

            def add_expert(k, e):
                t0, t1 = span(k)
                c0, c1 = t0 * P, t1 * P
                pool.wait_ge(gate_done, E * k + e + 1)
                if e == 1:
                    wait(pool, out_turned, k)
                    g.tensor_tensor(acc[:, c0:c1], gated[:, 0, c0:c1], gated[:, 1, c0:c1], ALU.add).then_inc(acc_added, 1)
                else:
                    pool.wait_ge(acc_added, ADDS * k + e - 1)
                    g.tensor_tensor(acc[:, c0:c1], acc[:, c0:c1], gated[:, e % 2, c0:c1], ALU.add).then_inc(acc_added, 1)

            def out_affine(k):
                t0, t1 = span(k)
                pool.wait_ge(ln_o, 4 * k + 4)
                if k_is0(k):
                    pool.wait_ge(scaled, 2)
                gb = gamma_h[:, :].rearrange("p (a d) -> p a d", a=1).to_broadcast([P, t1 - t0, D])
                bb = beta_h[:, :].rearrange("p (a d) -> p a d", a=1).to_broadcast([P, t1 - t0, D])
                g.tensor_tensor(on[:, t0:t1], on[:, t0:t1], gb, ALU.mult).then_inc(affine, 1)
                pool.wait_ge(affine, 2 * k + 1)
                g.tensor_tensor(on[:, t0:t1], on[:, t0:t1], bb, ALU.add).then_inc(affine, 1)

            def k_is0(k):
                return isinstance(k, int) and k == 0

            def body(k):
                c1, c2, c3 = k - 1, k - 2, k - 3
                for e in range(E):
                    if chunk_ok(c3):
                        add_state(c3, N_A + e - 1)
                    if e == 1 and unit_ok(k - 1):
                        rstd_unit(k - 1, o_ve, o_rs, ln_o, rstd_o)
                    if e == 3 and unit_ok(k - 1):
                        out_affine(k - 1)
                for e in range(E):
                    if e == 0 and chunk_ok(c1):
                        pool.wait_ge(ln_m, 4 * c1 + 3)
                        g.tensor_tensor(m_rs[:, :], m_ve[:, :], mhalf[:, 0:TT], ALU.pow).then_inc(rstd_m, 1)
                    if e >= 1 and unit_ok(k):
                        add_expert(k, e)
                    if chunk_ok(c2):
                        for n in N_OF[e]:
                            if n >= 1:
                                add_state(c2, n - 1)
                    if e == 3 and unit_ok(k + 1):
                        rstd_unit(k + 1, f_ve, f_rs, ln_f, rstd_f)

            rstd_unit(0, f_ve, f_rs, ln_f, rstd_f)
            over_units(pool, body)

        @block.vector
        def _(dve):
            v = nc.vector

            for e in range(E):
                last = v.memset(rank[:, :, e:e + 1], float(E - e))
            last.then_inc(consts_made, 1)
            n_split = [0]

            def split(hi, lo, src):
                v.tensor_copy(hi, src).then_inc(split_made, 1)
                n_split[0] += 1
                dve.wait_ge(split_made, n_split[0])
                v.tensor_tensor(lo, src, hi.bitcast(F32), ALU.subtract).then_inc(split_made, 1)
                n_split[0] += 1

            def carry_wait():
                v.memset(spare[:, :], 0.0)

            def ln_stats(src, tiles, st, done, count):
                carry_wait()
                for j in tiles:
                    last = v.bn_stats(st[:, j, :], src(j))
                last.then_inc(done, 1)
                dve.wait_ge(done, count + 1)
                carry_wait()

            def ln_moments(tiles, st, mv, ve, done, count):
                for j in tiles:
                    last = v.bn_aggr(mv[:, j, :], st[:, j, :])
                last.then_inc(done, 1)
                dve.wait_ge(done, count + 2)
                t0, t1 = tiles[0], tiles[-1] + 1
                v.tensor_scalar(ve[:, t0:t1], mv[:, t0:t1, 1:2].rearrange("p a b -> p (a b)"), EPS_LN, None,
                                ALU.add).then_inc(done, 1)

            def ln_apply(src, dst, tiles, mv, rs, done):
                for j in tiles:
                    last = v.tensor_scalar(dst[:, j, :], src(j), mv[:, j, 0:1], rs[:, j:j + 1],
                                           ALU.subtract, ALU.mult)
                last.then_inc(done, 1)

            def pre_norm(k):
                tiles = range(*span(k))
                if isinstance(k, int) and k == 0:
                    dve.wait_ge(ld_x, 16 * NB * TT)
                if parts(k)[1]:
                    wait(dve, mamba_added, k - LAG + 1)
                ln_stats(lambda j: x_tile(k, j), tiles, f_st, ln_f, 4 * k)
                ln_moments(tiles, f_st, f_mv, f_ve, ln_f, 4 * k)

            def pre_apply(k):
                tiles = range(*span(k))
                dve.wait_ge(rstd_f, k + 1)
                wait(dve, x_turned, k)
                ln_apply(lambda j: x_tile(k, j), xn, tiles, f_mv, f_rs, ln_f)

            def pre_split(k):
                t0, t1 = span(k)
                c0, c1 = t0 * P, t1 * P
                dve.wait_ge(x_turned, k + 1)
                wait(dve, work_full, WORK * (k - 1) + E * M)
                if isinstance(k, int) and k == 0:
                    v.tensor_copy(x_hi[:, c0:c1], f_bank[:, c0:c1]).then_inc(x_split, 1)
                dve.wait_ge(x_split, 2 * k + 1)
                v.tensor_tensor(x_lo[:, c0:c1], f_bank[:, c0:c1], x_hi[:, c0:c1].bitcast(F32),
                                ALU.subtract).then_inc(x_split, 1)

            def router(k, i):
                t0, t1 = span(k)
                nt = t1 - t0
                cut = slice(t0, t1)

                def wide(t):
                    return t[:, cut].rearrange("p (a b) -> p a b", b=1).to_broadcast([P, nt, E])

                if i == 0:
                    dve.wait_ge(logits_made, k + 1)
                    bgw = bg_sb[:, :].rearrange("p (a e) -> p a e", a=1).to_broadcast([P, nt, E])
                    made = v.tensor_tensor(lg[:, cut], f_bank[:, t0 * E:t1 * E].rearrange("p (a e) -> p a e", e=E),
                                           bgw, ALU.add)
                    made.then_inc(route, 1)
                    return
                dve.wait_ge(route, ROUTE * k + i)
                if i == 1:
                    made = v.tensor_reduce(top[:, cut], lg[:, cut], AX, ALU.max)
                elif i == 2:
                    wait(dve, tanhs, k)
                    made = v.tensor_tensor(sh[:, cut], lg[:, cut], wide(top), ALU.subtract)
                elif i == 3:
                    made = v.tensor_tensor(eq[:, cut], lg[:, cut], wide(top), ALU.is_equal)
                elif i == 4:
                    made = v.tensor_tensor(eq[:, cut], eq[:, cut], rank[:, cut], ALU.mult)
                elif i == 5:
                    made = v.tensor_reduce(best[:, cut], eq[:, cut], AX, ALU.max)
                elif i == 6:
                    made = v.tensor_tensor(first[:, cut], eq[:, cut], wide(best), ALU.is_equal)
                elif i == 7:
                    made = v.scalar_tensor_tensor(lg2[:, cut], first[:, cut], FAR, lg[:, cut], ALU.mult, ALU.add)
                elif i == 8:
                    made = v.tensor_reduce(top[:, cut], lg2[:, cut], AX, ALU.max)
                elif i == 9:
                    made = v.tensor_tensor(eq[:, cut], lg2[:, cut], wide(top), ALU.is_equal)
                elif i == 10:
                    made = v.tensor_tensor(eq[:, cut], eq[:, cut], rank[:, cut], ALU.mult)
                elif i == 11:
                    made = v.tensor_reduce(best[:, cut], eq[:, cut], AX, ALU.max)
                elif i == 12:
                    made = v.tensor_tensor(both[:, cut], eq[:, cut], wide(best), ALU.is_equal)
                elif i == 13:
                    made = v.tensor_tensor(both[:, cut], both[:, cut], first[:, cut], ALU.add)
                elif i == 14:
                    dve.wait_ge(tanhs, k + 1)
                    made = v.tensor_scalar(eq[:, cut], ex[:, cut], -1.0, 1.0, ALU.mult, ALU.add)
                elif i == 15:
                    made = v.reciprocal(eq[:, cut], eq[:, cut])
                elif i == 16:
                    made = v.scalar_tensor_tensor(ex[:, cut], ex[:, cut], 1.0, eq[:, cut], ALU.add, ALU.mult)
                elif i == 17:
                    made = v.tensor_tensor(num[:, cut], ex[:, cut], both[:, cut], ALU.mult)
                elif i == 18:
                    made = v.tensor_reduce(whole[:, cut], ex[:, cut], AX, ALU.add)
                elif i == 19:
                    made = v.tensor_reduce(den[:, cut], num[:, cut], AX, ALU.add)
                elif i == 20:
                    made = v.scalar_tensor_tensor(den[:, cut], whole[:, cut], EPS_GATE, den[:, cut], ALU.mult, ALU.add)
                elif i == 21:
                    made = v.reciprocal(den[:, cut], den[:, cut])
                else:
                    wait(dve, cw_turned, k)
                    made = v.tensor_tensor(cw[:, cut], num[:, cut], wide(den), ALU.mult)
                made.then_inc(route, 1)

            def cw_copy(k):
                t0, t1 = span(k)
                c0, c1 = t0 * P, t1 * P
                dve.wait_ge(cw_turned, k + 1)
                wait(dve, cw_stored, 16 * k)
                wait(dve, out_turned, k)
                v.tensor_copy(cwT[:, c0:c1], f_bank[0:E, c0:c1]).then_inc(cwT_made, 1)

            def gate(k, e):
                t0, t1 = span(k)
                c0, c1 = t0 * P, t1 * P
                dve.wait_ge(work_full, WORK * k + E * M + e + 1)
                if e % SPREAD == 0:
                    dve.wait_ge(cw_spread[e // SPREAD], 16 * k + 16)
                wait(dve, acc_added, ADDS * k + (max(1, e - 2) if e >= 2 else 0))
                v.tensor_tensor(gated[:, e % 2, c0:c1], work[e % WB][:, c0:c1], cwB[:, e, c0:c1],
                                ALU.mult).then_inc(gate_done, 1)

            def out_norm(k):
                tiles = range(*span(k))
                dve.wait_ge(out_turned, k + 1)
                ln_stats(lambda j: f_bank[:, j * D:(j + 1) * D], tiles, o_st, ln_o, 4 * k)
                ln_moments(tiles, o_st, o_mv, o_ve, ln_o, 4 * k)

            def out_apply(k):
                tiles = range(*span(k))
                dve.wait_ge(rstd_o, k + 1)
                ln_apply(lambda j: f_bank[:, j * D:(j + 1) * D], on, tiles, o_mv, o_rs, ln_o)

            def out_add(k):
                f1, f2 = parts(k)
                dve.wait_ge(affine, 2 * k + 2)
                if f1:
                    v.tensor_tensor(x_chunk(k), x_chunk(k), on[:, 0:TT], ALU.add).then_inc(ffn1_added, 1)
                if f2:
                    v.tensor_tensor(x_chunk(k - LAG), x_chunk(k - LAG), on[:, TT:2 * TT], ALU.add).then_inc(ffn2_added, 1)

            def m_tile(c):
                return lambda j: x_tile(c, j)

            def m_norm(c):
                dve.wait_ge(ffn1_added, c + 1)
                ln_stats(m_tile(c), range(TT), m_st, ln_m, 4 * c)
                ln_moments(range(TT), m_st, m_mv, m_ve, ln_m, 4 * c)

            def m_apply(c):
                dve.wait_ge(rstd_m, c + 1)
                wait(dve, dt_made, c)
                ln_apply(m_tile(c), xm, range(TT), m_mv, m_rs, ln_m)

            def m_split(c):
                dve.wait_ge(xm_turned, c + 1)
                wait(dve, inz_made, c)
                dve.wait_ge(xm_split, 2 * c + 1)
                v.tensor_tensor(xm_lo[:, :], m_bank[:, 0:CT], xm_hi[:, :].bitcast(F32), ALU.subtract).then_inc(xm_split, 1)

            def m_halo(c):
                dve.wait_ge(xpad_made, c + 1)
                v.tensor_copy(xpad[:, :, 0:KC - 1], halo[:, 0]).then_inc(halo_set, 1)
                dve.wait_ge(halo_set, 3 * c + 1)
                v.tensor_copy(halo[:, 0], halo[:, 1]).then_inc(halo_set, 1)
                dve.wait_ge(halo_set, 3 * c + 2)
                v.tensor_copy(halo[:, 1], xpad[:, :, CT:CT + KC - 1]).then_inc(halo_set, 1)

            def m_carry(c):
                dve.wait_ge(carry_kept, NS * c + NS)
                v.tensor_copy(carry[:, 0], carry[:, 1]).then_inc(carry_moved, 1)
                dve.wait_ge(carry_moved, 2 * c + 1)
                v.tensor_copy(carry[:, 1], carry_new[:, :, :]).then_inc(carry_moved, 1)

            def m_conv(c, routes=()):
                for t in range(KC - 1):
                    for step in routes[2 * t:2 * t + 1]:
                        router(*step)
                    dve.wait_ge(conv, KC * c + t + 1)
                    for h in range(H):
                        last = v.scalar_tensor_tensor(u[:, h], xpad[:, h, t:t + CT], convw_sb[:, h, t:t + 1],
                                                      u[:, h], ALU.mult, ALU.add)
                        if h == 0:
                            for step in routes[2 * t + 1:2 * t + 2]:
                                router(*step)
                    last.then_inc(conv, 1)

            def m_silu(c, of_z):
                if of_z:
                    dve.wait_ge(z_read, 2 * c + 2)
                else:
                    dve.wait_ge(x_tanhed, c + 1)
                a = flat((zs_next if of_z else u)[:, :, :])
                v.scalar_tensor_tensor(a, z_tanh if of_z else x_tanh, 1.0, a, ALU.add, ALU.mult).then_inc(silu, 1)

            def m_xdbl(c):
                dve.wait_ge(xdbl_read, 3 * c + 2)
                v.tensor_tensor(bc[2 * NS:4 * NS, :], m_bank[R:R + 2 * NS, 0:CT],
                                bc[0:2 * NS, :].bitcast(F32), ALU.subtract).then_inc(xdbl_read, 1)

            def m_softplus(c):
                base = [SPD * c]

                def step(ins):
                    ins.then_inc(sp_dve, 1)
                    base[0] = base[0] + 1
                    dve.wait_ge(sp_dve, base[0])

                dve.wait_ge(sp_act, SPA * c + 2)
                step(v.scalar_tensor_tensor(flat(sp_s4), flat(sp_tanh), 1.0, flat(sp_exp), ALU.add, ALU.mult))
                dve.wait_ge(sp_act, SPA * c + 4)
                step(v.tensor_scalar(flat(sp_b), flat(sp_b), LEAD / 4, B0 * LEAD / 4, ALU.mult, ALU.add))
                dve.wait_ge(sp_act, SPA * c + 5)
                step(v.scalar_tensor_tensor(flat(sp_b), flat(sp_a), A0, flat(sp_b), ALU.add, ALU.mult))
                step(v.tensor_tensor(flat(sp_b), flat(sp_b), flat(sp_s4), ALU.mult))
                dve.wait_ge(dt_read, 2 * c + 2)
                wait(dve, decay_made, NS * c)
                step(v.tensor_tensor(flat(dt[:, :, :]), flat(sp_b), flat(sp_pos), ALU.add))
                v.tensor_tensor(flat(dtu[:, :, :]), flat(dt[:, :, :]), flat(u[:, :, :]), ALU.mult).then_inc(sp_dve, 1)

            def m_state(c, n, routes=()):
                if n < NS:
                    dve.wait_ge(bc_spread, NS * c + n + 1)
                    if n == 0:
                        dve.wait_ge(sp_dve, SPD * c + SPD)
                    if n >= 2:
                        dve.wait_ge(scanned, NS * c + n - 1)
                    v.tensor_tensor(drive[:, n % 2], dtu[:, :, :], bc_wide(n, 0), ALU.mult).then_inc(drive_made, 1)
                for step in routes[0:1]:
                    router(*step)
                if n >= 1:
                    dve.wait_ge(scanned, NS * c + n)
                    wait(dve, y_added, NS * c + n - 2)
                    v.tensor_tensor(seen[:, (n - 1) % 2], state[:, (n - 1) % 2], bc_wide(n - 1, 1),
                                    ALU.mult).then_inc(seen_made, 1)
                for step in routes[1:2]:
                    router(*step)
                if n < NS:
                    dve.wait_ge(drive_made, NS * c + n + 1)
                    dve.wait_ge(decay_made, NS * c + n + 1)
                    wait(dve, carry_kept, NS * c + n - 1)
                    if n >= 2:
                        dve.wait_ge(seen_made, NS * c + n - 1)
                    if n == 0:
                        wait(dve, carry_moved, 2 * c)
                    for h in range(H):
                        last = v.tensor_tensor_scan(state[:, n % 2, h], decay[:, n % NSLOT, h], drive[:, n % 2, h],
                                                    carry[:, 0, h, n:n + 1], ALU.mult, ALU.add)
                        if h == 0:
                            for step in routes[2:3]:
                                router(*step)
                    last.then_inc(scanned, 1)
                for step in routes[3:]:
                    router(*step)

            def m_gate(c):
                dve.wait_ge(y_added, NS * c + NS)
                dve.wait_ge(begun, 2 * c + 2)
                v.tensor_tensor(flat(y_acc[:, :, :]), flat(y_acc[:, :, :]), flat(zs[:, :, :]), ALU.mult).then_inc(y_gated, 1)

            def m_add(c):
                dve.wait_ge(mamba_made, c + 1)
                v.tensor_tensor(x_chunk(c), x_chunk(c), m_bank[:, 0:TT * D].rearrange("p (a d) -> p a d", d=D),
                                ALU.add).then_inc(mamba_added, 1)

            dve.wait_ge(ld_vec, 16 * 6)
            split(wg_hi[:, :], wg_lo[:, :], hid[:, E, 0:E])
            pre_norm(0)
            dve.wait_ge(consts_made, 1)
            dve.wait_ge(pool_setup, 2)
            pre_apply(0)
            for e in range(2):
                dve.wait_ge(ld_w1[e], 16)
                split(w1_hi[:, e], w1_lo[:, e], hid[:, e, :])
            pre_split(0)
            for i in range(14):
                router(0, i)
            for e in range(2, E):
                dve.wait_ge(ld_w1[e], 16)
                split(w1_hi[:, e], w1_lo[:, e], hid[:, e, :])
            dve.wait_ge(ld_mamba, 16 * 8)
            split(win_hi[:, :], win_lo[:, :], hid[:, E + 1, 0:2 * DI])
            dve.wait_ge(cols_turned, 1)
            v.tensor_copy(cols[:, :], m_bank[:, 0:ROWS]).then_inc(cols_made, 1)
            dve.wait_ge(cols_made, 1)
            v.tensor_scalar(convb_col, convb_col, 0.5, None, ALU.mult)
            v.tensor_scalar(flat(convw_sb[:, :, :]), flat(convw_sb[:, :, :]), 0.5, None, ALU.mult)
            v.tensor_scalar(gamma_h[:, :], gamma_h[:, :], 0.5, None, ALU.mult).then_inc(scaled, 1)
            v.tensor_scalar(beta_h[:, :], beta_h[:, :], 0.5, None, ALU.mult).then_inc(scaled, 1)
            dve.wait_ge(ident_made, 1)
            v.tensor_copy(pick[0:2 * NS, :], ident[0:2 * NS, 0:2 * NS])
            v.tensor_copy(pick[2 * NS:4 * NS, :], ident[2 * NS:4 * NS, 2 * NS:4 * NS]).then_inc(cols_made, 1)
            dve.wait_ge(a_exp, 1)
            v.tensor_scalar(flat(a_neg[:, :, :]), flat(a_neg[:, :, :]), -1.0, None, ALU.mult).then_inc(cols_made, 1)
            for i in range(14, ROUTE):
                router(0, i)
            def body(k):
                c1, c2, c3 = k - 1, k - 2, k - 3
                for e in range(E):
                    routes = [(k, i) for i in ROUTES[e]] if unit_ok(k) and not (isinstance(k, int) and k == 0) else []
                    state_routes, other_routes = routes[:4], routes[4:]
                    if e == 5 and unit_ok(k):
                        cw_copy(k)
                    if chunk_ok(c2):
                        if e == 4:
                            m_silu(c2, False)
                        if e == 6:
                            m_xdbl(c2)
                    if chunk_ok(c3):
                        m_state(c3, N_A + e, state_routes)
                    else:
                        for step in state_routes:
                            router(*step)
                    if e == 0 and chunk_ok(c2):
                        m_halo(c2)
                        m_conv(c2, other_routes)
                    else:
                        if e == 2 and chunk_ok(c2):
                            m_silu(c2, True)
                        for step in other_routes:
                            router(*step)
                    if e == 1 and unit_ok(k - 1):
                        out_norm(k - 1)
                    if e == 2 and unit_ok(k - 1):
                        out_apply(k - 1)
                    if e == 4 and unit_ok(k - 1):
                        out_add(k - 1)
                for e in range(E):
                    if unit_ok(k):
                        gate(k, e)
                    if e == 0 and chunk_ok(c3):
                        m_gate(c3)
                    if e == 0 and chunk_ok(c1):
                        m_norm(c1)
                    if e == 0 and chunk_ok(c2):
                        m_softplus(c2)
                    if e == 2:
                        if chunk_ok(c3):
                            m_add(c3)
                            m_carry(c3)
                    if e == 1 and chunk_ok(c1):
                        m_apply(c1)
                    if e == 4 and chunk_ok(c1):
                        m_split(c1)
                    if unit_ok(k + 1):
                        if e == 3:
                            pre_norm(k + 1)
                        if e == 4:
                            pre_apply(k + 1)
                        if e == 6:
                            pre_split(k + 1)
                    if chunk_ok(c2):
                        for n in N_OF[e]:
                            m_state(c2, n)

            over_units(dve, body)

        @block.scalar
        def _(act):
            s = nc.scalar
            act.dma_start(gamma_h[:, :], gamma.rearrange("(a e) -> a e", a=1).to_broadcast([P, D])).then_inc(ld_mamba, 16)
            act.dma_start(beta_h[:, :], beta.rearrange("(a e) -> a e", a=1).to_broadcast([P, D])).then_inc(ld_mamba, 16)
            act.dma_start(a_neg[:, :, :], a_log.rearrange("(h p) n -> p h n", p=P)).then_inc(ld_mamba, 16)
            act.dma_start(convw_sb[:, :, :], conv_w.rearrange("(h p) n -> p h n", p=P)).then_inc(ld_mamba, 16)
            act.dma_start(b2_sb[:, :], b2).then_inc(ld_w2, 16)
            for e in range(E):
                act.dma_start(w2[:, e], W2[e].rearrange("(m p) d -> p m d", p=P)).then_inc(ld_w2, 16)
            act.wait_ge(ld_mamba, 16 * 8)
            s.activation(flat(a_neg[:, :, :]), flat(a_neg[:, :, :]), ACT.Exp).then_inc(a_exp, 1)
            act.wait_ge(cols_made, 1)

            def gelu(k, e, m):
                t0, t1 = span(k)
                c0, c1 = t0 * P, t1 * P
                i = e * M + m
                act.wait_ge(work_full, WORK * k + i + 1)
                if isinstance(k, int) and k == 0 and i == 0:
                    act.wait_ge(split_made, 2 * (E + 2))
                s.activation(hid[:, i, c0:c1], work[i % WB][:, c0:c1], ACT.Gelu,
                             bias=b1_col[:, i:i + 1]).then_inc(gelu_done, 1)

            def softmax_tanh(k):
                t0, t1 = span(k)
                act.wait_ge(route, ROUTE * k + 3)
                s.activation(ex[:, t0:t1], sh[:, t0:t1], ACT.Tanh, scale=0.5).then_inc(tanhs, 1)

            def m_xin(c):
                act.wait_ge(inx_made, c + 1)
                wait(act, conv, KC * c)
                wait(act, halo_set, 3 * c)
                s.activation(xpad[:, :, KC - 1:], m_bank[:, :].rearrange("p (h t) -> p h t", h=H),
                             ACT.Copy).then_inc(xpad_made, 1)
                wait(act, sp_dve, SPD * c)
                for h in range(H):
                    last = s.activation(u[:, h], m_bank[:, h * CT:(h + 1) * CT], ACT.Identity,
                                        scale=convw_sb[:, h, KC - 1:KC], bias=convb_col[:, h:h + 1])
                last.then_inc(conv, 1)

            def m_zin(c):
                act.wait_ge(inz_made, c + 1)
                wait(act, begun, 2 * c)
                s.activation(flat(zs_next[:, :, :]), m_bank[:, :], ACT.Copy, scale=0.5).then_inc(z_read, 1)
                wait(act, acc_added, ADDS * (c + 2))
                s.activation(z_tanh, m_bank[:, :], ACT.Tanh, scale=0.5).then_inc(z_read, 1)

            def m_xtanh(c):
                act.wait_ge(conv, KC * c + KC)
                s.activation(x_tanh, flat(u[:, :, :]), ACT.Tanh).then_inc(x_tanhed, 1)

            def m_xdbl(c):
                act.wait_ge(xdbl_made, c + 1)
                s.activation(dt_low, m_bank[0:R, 0:CT], ACT.Copy).then_inc(xdbl_read, 1)
                wait(act, bc_spread, NS * c)
                s.activation(bc[0:2 * NS, :], m_bank[R:R + 2 * NS, 0:CT], ACT.Copy).then_inc(xdbl_read, 1)

            def m_pre(c):
                act.wait_ge(dt_made, c + 1)
                if isinstance(c, int) and c == 0:
                    act.wait_ge(pool_setup, 2)
                wait(act, scanned, NS * c - 1)
                for h in range(H):
                    src = m_bank[:, h * CT:(h + 1) * CT]
                    last = s.activation(sp_abs[:, h], src, ACT.Abs, bias=dtb_col[:, h:h + 1])
                last.then_inc(dt_read, 1)
                for h in range(H):
                    src = m_bank[:, h * CT:(h + 1) * CT]
                    last = s.activation(sp_pos[:, h], src, ACT.Relu, bias=dtb_col[:, h:h + 1])
                last.then_inc(dt_read, 1)

            def m_softplus(c):
                act.wait_ge(dt_read, 2 * c + 1)
                f1, f2 = parts(c + 1)
                if f2:
                    act.wait_ge(ffn2_added, c + 2 - LAG)
                else:
                    act.wait_ge(ffn1_added, c + 2)
                s.activation(flat(sp_exp), flat(sp_abs), ACT.Exp, scale=-1.0).then_inc(sp_act, 1)
                s.activation(flat(sp_tanh), flat(sp_abs), ACT.Tanh, scale=0.5, bias=sp_bias[:, 0:1]).then_inc(sp_act, 1)
                act.wait_ge(sp_dve, SPD * c + 1)
                s.activation(flat(sp_sq), flat(sp_s4), ACT.Square, scale=0.25).then_inc(sp_act, 1)
                act.wait_ge(sp_act, SPA * c + 3)
                s.activation(flat(sp_b), flat(sp_sq), ACT.Square, bias=sp_bias[:, 2:3]).then_inc(sp_act, 1)
                s.activation(flat(sp_a), flat(sp_sq), ACT.Square, bias=sp_bias[:, 1:2]).then_inc(sp_act, 1)

            def m_begin(c):
                wait(act, mamba_made, c)
                for h in range(H):
                    last = s.activation(y_acc[:, h], u[:, h], ACT.Copy, scale=dpar_col[:, h:h + 1])
                last.then_inc(begun, 1)
                s.activation(flat(zs[:, :, :]), flat(zs_next[:, :, :]), ACT.Copy).then_inc(begun, 1)

            def x_high(k):
                t0, t1 = span(k)
                c0, c1 = t0 * P, t1 * P
                act.wait_ge(x_turned, k + 1)
                wait(act, work_full, WORK * (k - 1) + E * M)
                s.activation(x_hi[:, c0:c1], f_bank[:, c0:c1], ACT.Copy).then_inc(x_split, 1)

            def m_high(c):
                act.wait_ge(xm_turned, c + 1)
                wait(act, inz_made, c)
                s.activation(xm_hi[:, :], m_bank[:, 0:CT], ACT.Copy).then_inc(xm_split, 1)

            def decays(c, n):
                if n == 0:
                    act.wait_ge(sp_dve, SPD * c + SPD - 1)
                wait(act, scanned, NS * c + n - NSLOT + 1)
                for h in range(H):
                    last = s.activation(decay[:, n % NSLOT, h], dt[:, h], ACT.Exp, scale=a_neg[:, h, n:n + 1])
                last.then_inc(decay_made, 1)

            def body(k):
                c1, c2 = k - 1, k - 2
                for e in range(E):
                    if unit_ok(k):
                        for m in range(M):
                            gelu(k, e, m)
                    if e == 0 and unit_ok(k):
                        softmax_tanh(k)
                    if chunk_ok(c2):
                        if e == 1:
                            m_zin(c2)
                        if e == 6:
                            m_xdbl(c2)
                        if e == 3:
                            m_xtanh(c2)
                        if e == 7:
                            m_pre(c2)
                if chunk_ok(c2):
                    m_softplus(c2)
                    for n in range(2):
                        decays(c2, n)
                    m_begin(c2)
                    for n in range(2, N_HIGH):
                        decays(c2, n)
                if chunk_ok(c1):
                    m_high(c1)
                if chunk_ok(c2):
                    for n in range(N_HIGH, N_X):
                        decays(c2, n)
                if unit_ok(k + 1):
                    x_high(k + 1)
                if chunk_ok(c2):
                    for n in range(N_X, N_XIN):
                        decays(c2, n)
                if chunk_ok(c1):
                    m_xin(c1)
                if chunk_ok(c2):
                    for n in range(N_XIN, NS):
                        decays(c2, n)

            over_units(act, body)

        @block.tensor
        def _(pe):
            t = nc.tensor

            def three(dst, hi_w, lo_w, hi_x, lo_x):
                t.matmul(dst, hi_w, hi_x, start=True, stop=False)
                t.matmul(dst, hi_w, lo_x, start=False, stop=False)
                return t.matmul(dst, lo_w, hi_x, start=False, stop=True)

            def last_use(uses, i):
                return max(j for j in range(uses) if j % WB == i)

            def turn_x(k):
                pe.wait_ge(ln_f, 4 * k + 4)
                wait(pe, cwT_made, k)
                for j in range(*span(k)):
                    last = t.transpose(f_bank[:, j * P:(j + 1) * P], xn[:, j, :], ident[:, :])
                last.then_inc(x_turned, 1)

            def logits(k):
                pe.wait_ge(x_split, 2 * k + 2)
                for j in range(*span(k)):
                    xh, xl = x_hi[:, j * P:(j + 1) * P], x_lo[:, j * P:(j + 1) * P]
                    dst = f_bank[:, j * E:(j + 1) * E]
                    t.matmul(dst, xh, wg_hi[:, :], start=True, stop=False)
                    t.matmul(dst, xh, wg_lo[:, :], start=False, stop=False)
                    last = t.matmul(dst, xl, wg_hi[:, :], start=False, stop=True)
                last.then_inc(logits_made, 1)

            def turn_cw(k):
                pe.wait_ge(route, ROUTE * k + ROUTE)
                wait(pe, ln_o, 4 * k)
                for j in range(*span(k)):
                    last = t.transpose(f_bank[0:E, j * P:(j + 1) * P], cw[:, j, :], ident[:, :])
                last.then_inc(cw_turned, 1)

            def w1(k, e, m):
                t0, t1 = span(k)
                c0, c1 = t0 * P, t1 * P
                i = e * M + m
                if isinstance(k, int) and k == 0 and m == 0:
                    pe.wait_ge(split_made, 2 * (e + 2))
                if i < WB:
                    wait(pe, gate_done, E * (k - 1) + last_use(E, i) + 1)
                else:
                    pe.wait_ge(gelu_done, E * M * k + i - WB + 1)
                cut = slice(m * P, (m + 1) * P)
                three(work[i % WB][:, c0:c1], w1_hi[:, e, cut], w1_lo[:, e, cut],
                      x_hi[:, c0:c1], x_lo[:, c0:c1]).then_inc(work_full, 1)

            def w2_(k, e):
                t0, t1 = span(k)
                c0, c1 = t0 * P, t1 * P
                if e < WB:
                    pe.wait_ge(gelu_done, E * M * k + last_use(E * M, e) + 1)
                else:
                    pe.wait_ge(gate_done, E * k + e - WB + 1)
                if isinstance(k, int) and k == 0 and e == 0:
                    pe.wait_ge(ld_w2, 16 * (E + 1))
                for m in range(M):
                    last = t.matmul(work[e % WB][:, c0:c1], w2[:, e, m, :], hid[:, e * M + m, c0:c1],
                                    start=m == 0, stop=m == M - 1)
                last.then_inc(work_full, 1)

            def turn_out(k):
                pe.wait_ge(acc_added, ADDS * k + ADDS)
                if unit_ok(k + 1):
                    pe.wait_ge(route, ROUTE * (k + 1) + 1)
                for j in range(*span(k)):
                    dst = f_bank[:, j * D:(j + 1) * D]
                    t.matmul(dst, acc[:, j * P:(j + 1) * P], ident[:, :], start=True, stop=False)
                    last = t.matmul(dst, cwT[:, j * P:(j + 1) * P], b2_sb[:, :], start=False, stop=True)
                last.then_inc(out_turned, 1)

            def turn_xm(c):
                pe.wait_ge(ln_m, 4 * c + 4)
                wait(pe, mamba_added, c - 1)
                for j in range(TT):
                    last = t.transpose(m_bank[:, j * P:(j + 1) * P], xm[:, j, :], ident[:, :])
                last.then_inc(xm_turned, 1)

            def in_proj(c, z, done):
                pe.wait_ge(xm_split, 2 * c + 2)
                if z:
                    pe.wait_ge(conv, KC * c + 1)
                for h in range(H):
                    at = z * DI + h * P
                    last = three(m_bank[:, h * CT:(h + 1) * CT], win_hi[:, at:at + P], win_lo[:, at:at + P],
                                 xm_hi[:, :], xm_lo[:, :])
                last.then_inc(done, 1)

            def x_proj(c):
                pe.wait_ge(silu, 2 * c + 2)
                pe.wait_ge(z_read, 2 * c + 2)
                for h in range(H):
                    last = t.matmul(m_bank[0:R + 2 * NS, 0:CT], xp_sb[:, h, :], u[:, h, :], start=h == 0, stop=h == H - 1)
                last.then_inc(xdbl_made, 1)

            def dt_proj(c):
                pe.wait_ge(xdbl_read, 3 * c + 3)
                for h in range(H):
                    last = t.matmul(m_bank[:, h * CT:(h + 1) * CT], dtw_sb[:, h * P:(h + 1) * P], dt_low,
                                    start=True, stop=True)
                last.then_inc(dt_made, 1)

            def spread(c, n):
                pe.wait_ge(xdbl_read, 3 * c + 3)
                wait(pe, seen_made, NS * c + max(n - BB + 1, 0))
                bank = bc_bank[n % BB]
                for i, row in enumerate((n, NS + n)):
                    one = pick[:, row:row + 1].to_broadcast([4 * NS, P])
                    last = t.matmul(bank[:, i * CT:(i + 1) * CT], one, bc[:, :], start=True, stop=True)
                last.then_inc(bc_spread, 1)

            def out_proj(c):
                pe.wait_ge(y_gated, c + 1)
                if chunk_ok(c + 1):
                    pe.wait_ge(dt_read, 2 * (c + 1) + 2)
                for j in range(TT):
                    for h in range(H):
                        last = t.matmul(m_bank[:, j * D:(j + 1) * D], y_acc[:, h, j * P:(j + 1) * P], wout_sb[:, h, :],
                                        start=h == 0, stop=h == H - 1)
                last.then_inc(mamba_made, 1)

            pe.wait_ge(ident_made, 1)
            pe.wait_ge(ld_vec, 16 * 6)
            t.transpose(m_bank[:, 0:ROWS], rows, ident[0:ROWS, 0:ROWS]).then_inc(cols_turned, 1)
            turn_x(0)
            logits(0)

            def body(k):
                c1, c2, c3 = k - 1, k - 2, k - 3
                for e in range(E):
                    if e == 5 and unit_ok(k):
                        turn_cw(k)
                    if e == 0 and chunk_ok(c3):
                        spread(c3, N_A)
                    for m in range(M):
                        if unit_ok(k):
                            w1(k, e, m)
                        if m == 0 and e >= 1 and chunk_ok(c3) and N_A + e < NS:
                            spread(c3, N_A + e)
                    if e == 1 and unit_ok(k - 1):
                        turn_out(k - 1)
                    if not chunk_ok(c2):
                        continue
                    if e == 0:
                        in_proj(c2, 1, inz_made)
                    if e == 5:
                        x_proj(c2)
                    if e == 7:
                        dt_proj(c2)
                for e in range(E):
                    if unit_ok(k):
                        w2_(k, e)
                    if e == 2 and chunk_ok(c3):
                        out_proj(c3)
                    if chunk_ok(c2):
                        if e == 1:
                            pe.wait_ge(cols_made, 2)
                        for n in N_OF[e]:
                            spread(c2, n)
                    if chunk_ok(c1):
                        if e == 4:
                            turn_xm(c1)
                        if e == 6:
                            in_proj(c1, 0, inx_made)
                    if e == 5 and unit_ok(k + 1):
                        turn_x(k + 1)
                    if e == 7 and unit_ok(k + 1):
                        logits(k + 1)

            over_units(pe, body)


_INS = ["L0_attn_hidden_states", "L0_attn_in_proj_w", "L0_attn_conv_w", "L0_attn_conv_b", "L0_attn_x_proj_w",
        "L0_attn_dt_proj_w", "L0_attn_dt_bias", "L0_attn_A_log", "L0_attn_D_param", "L0_attn_out_proj_w",
        "L0_ffn_Wg", "L0_ffn_bg", "L0_ffn_W1", "L0_ffn_b1", "L0_ffn_W2", "L0_ffn_b2", "L0_ffn_gamma", "L0_ffn_beta"]


def kernel(**inputs):
    import numpy as np
    import concourse.bacc as bacc
    from concourse.bass_utils import run_bass_kernel_spmd

    nc = bacc.Bacc("TRN2", target_bir_lowering=False, num_devices=1)
    arrays, args = {}, []
    for name in _INS:
        a = np.ascontiguousarray(inputs[name])
        arrays[f"in_{name}"] = a
        args.append(nc.dram_tensor(f"in_{name}", a.shape, mybir.dt.from_np(a.dtype), kind="ExternalInput").ap())
    experts = arrays["in_L0_ffn_W1"].shape[0]
    args.append(nc.dram_tensor("gate_scratch", (experts, 2 * CT), F32, kind="Internal").ap())
    shape = arrays["in_L0_attn_hidden_states"].shape
    args.append(nc.dram_tensor("out", shape, F32, kind="ExternalOutput").ap())
    macaron(nc, *args)
    return run_bass_kernel_spmd(nc, [arrays], core_ids=[0]).results[0]["out"]
```

```python
from contextlib import ExitStack

import concourse.bass as bass
from concourse import mybir

F32 = mybir.dt.float32
F32R = mybir.dt.float32r
ALU = mybir.AluOpType
ACT = mybir.ActivationFunctionType
AX = mybir.AxisListType.X

P = 128
CT = 256
TT = CT // P
LAG = 4
EPS_LN = 1e-5
EPS_GATE = 1e-8
FAR = -3.0e38
NSLOT = 8
WB = 3
SPREAD = 2
BB = 3
HALF_LN2 = 0.34657359027997264
LEAD = 0.28174657258139
A1, A0 = 1.267423698171514, 1.1272198435930603
B1, B0 = -0.7712079220645582, 2.0020421682902847


def wait(eng, sem, value):
    if isinstance(value, int) and value <= 0:
        return
    eng.wait_ge(sem, value)


def macaron(nc, hidden, in_w, conv_w, conv_b, xp_w, dt_w, dt_b, a_log, d_par, out_w,
            Wg, bg, W1, b1, W2, b2, gamma, beta, cw_dram, out):
    NB, L, D = hidden.shape
    E, _, DFF = W1.shape
    M = DFF // P
    DI = in_w.shape[1] // 2
    H = DI // P
    NS = a_log.shape[1]
    KC = conv_w.shape[1]
    R = dt_w.shape[0]
    CHUNKS = NB * L // CT
    NT = CHUNKS * TT
    UNITS = CHUNKS + LAG
    LOOP = (LAG + 1, CHUNKS - 1)
    WORK = E * M + E
    ADDS = E - 1
    NB1 = E * M
    ROWS = NB1 + 3 * H

    with ExitStack() as ctx:
        def sb(name, shape, dt=F32):
            return ctx.enter_context(nc.sbuf_tensor(name, shape, dt))

        def sem(name):
            return ctx.enter_context(nc.semaphore(name))

        def flat(ap):
            return ap.rearrange("p a b -> p (a b)")

        w1_hi = sb("w1_hi", [P, E, DFF], F32R)
        w1_lo = sb("w1_lo", [P, E, DFF], F32R)
        w2 = sb("w2", [P, E, M, D])
        wg_hi = sb("wg_hi", [P, E], F32R)
        wg_lo = sb("wg_lo", [P, E], F32R)
        win_hi = sb("win_hi", [P, 2 * DI], F32R)
        win_lo = sb("win_lo", [P, 2 * DI], F32R)
        xp_sb = sb("xp_sb", [P, H, R + 2 * NS])
        dtw_sb = sb("dtw_sb", [R, DI])
        wout_sb = sb("wout_sb", [P, H, D])
        b2_sb = sb("b2_sb", [E, D])
        gamma_h = sb("gamma_h", [P, D])
        beta_h = sb("beta_h", [P, D])
        bg_sb = sb("bg_sb", [P, E])
        cols = sb("cols", [P, ROWS])
        convw_sb = sb("convw_sb", [P, H, KC])
        a_neg = sb("a_neg", [P, H, NS])
        ident = sb("ident", [P, P])
        pick = sb("pick", [2 * 2 * NS, 2 * NS], F32R)
        mhalf = sb("mhalf", [P, 2 * TT])
        rank = sb("rank", [P, 2 * TT, E])
        b1_col = cols[:, 0:NB1]
        convb_col = cols[:, NB1:NB1 + H]
        dtb_col = cols[:, NB1 + H:NB1 + 2 * H]
        dpar_col = cols[:, NB1 + 2 * H:ROWS]

        xs = sb("xs", [P, NT, D])
        hid = sb("hid", [P, E * M, 2 * CT])
        STAGED = E * M - E - 3
        w1_in = [hid[:, E * M - 1 - e, :] for e in range(E)]
        wg_in, win_in = hid[:, STAGED + 2, 0:E], hid[:, STAGED + 1, 0:2 * DI]
        rows = hid[0:ROWS, STAGED, 0:P]
        cwB = sb("cwB", [P, E, 2 * CT])
        cwT = sb("cwT", [E, 2 * CT])
        xn = sb("xn", [P, 2 * TT, D])
        x_hi = sb("x_hi", [P, 2 * CT], F32R)
        x_lo = sb("x_lo", [P, 2 * CT], F32R)
        gated = sb("gated", [P, 2, 2 * CT])
        acc = sb("acc", [P, 2 * CT])
        on = xn
        f_st = sb("f_st", [P, 2 * TT, 6])
        f_mv = sb("f_mv", [P, 2 * TT, 2])
        f_ve = sb("f_ve", [P, 2 * TT])
        f_rs = sb("f_rs", [P, 2 * TT])
        f_nm = sb("f_nm", [P, 2 * TT])
        o_st = sb("o_st", [P, 2 * TT, 6])
        o_mv = sb("o_mv", [P, 2 * TT, 2])
        o_ve = sb("o_ve", [P, 2 * TT])
        o_rs = sb("o_rs", [P, 2 * TT])
        o_nm = sb("o_nm", [P, 2 * TT])
        lg = sb("lg", [P, 2 * TT, E])
        lg2 = sb("lg2", [P, 2 * TT, E])
        sh = sb("sh", [P, 2 * TT, E])
        ex = sb("ex", [P, 2 * TT, E])
        num = lg2
        cw = sb("cw", [P, 2 * TT, E])
        eq = sb("eq", [P, 2 * TT, E])
        first = sb("first", [P, 2 * TT, E])
        both = sb("both", [P, 2 * TT, E])
        top = sb("top", [P, 2 * TT])
        best = sb("best", [P, 2 * TT])
        whole = sb("whole", [P, 2 * TT])
        den = sb("den", [P, 2 * TT])
        spare = sb("spare", [P, 1])
        sp_bias = sb("sp_bias", [P, 3])

        xm = sb("xm", [P, TT, D])
        xm_hi = sb("xm_hi", [P, CT], F32R)
        xm_lo = sb("xm_lo", [P, CT], F32R)
        m_st = sb("m_st", [P, TT, 6])
        m_mv = sb("m_mv", [P, TT, 2])
        m_ve = sb("m_ve", [P, TT])
        m_rs = sb("m_rs", [P, TT])
        m_nm = sb("m_nm", [P, TT])
        xpad = sb("xpad", [P, H, KC - 1 + CT])
        halo = sb("halo", [P, 2, H, KC - 1])
        u = sb("u", [P, H, CT])
        zs_next = sb("zs_next", [P, H, CT])
        z_tanh, x_tanh = gated[:, 0], gated[:, 1]
        zs = sb("zs", [P, H, CT])
        dt_low = flat(xm[:, :, :])[0:R]
        bc = sb("bc", [4 * NS, CT], F32R)
        dt = sb("dt", [P, H, CT])
        dtu = sb("dtu", [P, H, CT])
        decay = sb("decay", [P, NSLOT, H, CT])
        drive = sb("drive", [P, 2, H, CT])
        state = sb("state", [P, 2, H, CT])
        seen = sb("seen", [P, 2, H, CT])
        y_acc = sb("y_acc", [P, H, CT])
        carry = sb("carry", [P, 2, H, NS])
        carry_new = sb("carry_new", [P, H, NS])

        sp_abs = acc[:, :].rearrange("p (h t) -> p h t", h=H)
        sp_exp = xn[:, :, :].rearrange("p (h r) d -> p h (r d)", h=H)
        sp_pos, sp_tanh, sp_b = dt[:, :, :], sp_abs, sp_abs
        sp_s4, sp_sq = sp_exp, xpad[:, :, KC - 1:]
        sp_a = sp_sq

        work = [ctx.enter_context(nc.psum_tensor(f"work{i}", [P, 512], F32)) for i in range(WB)]
        f_bank = ctx.enter_context(nc.psum_tensor("f_bank", [P, 512], F32))
        m_bank = ctx.enter_context(nc.psum_tensor("m_bank", [P, 512], F32))
        bc_bank = [ctx.enter_context(nc.psum_tensor(f"bc_bank{i}", [P, 512], F32)) for i in range(BB)]

        ld_x0 = sem("ld_x0")
        ld_x = sem("ld_x")
        ld_w1 = [sem(f"ld_w1_{e}") for e in range(E)]
        ld_w2 = sem("ld_w2")
        ld_vec = sem("ld_vec")
        ld_mamba = sem("ld_mamba")
        consts_made = sem("consts_made")
        ident_made = sem("ident_made")
        pool_setup = sem("pool_setup")
        split_made = sem("split_made")
        cols_turned = sem("cols_turned")
        cols_made = sem("cols_made")
        a_made = sem("a_made")
        scaled = sem("scaled")
        ln_f = sem("ln_f")
        rstd_f = sem("rstd_f")
        applied_f = sem("applied_f")
        x_turned = sem("x_turned")
        x_split = sem("x_split")
        logits_made = sem("logits_made")
        route = sem("route")
        tanhs = sem("tanhs")
        cw_turned = sem("cw_turned")
        cwT_made = sem("cwT_made")
        cw_stored = sem("cw_stored")
        cw_spread = [sem(f"cw_spread_{i}") for i in range(E // SPREAD)]
        work_full = sem("work_full")
        gelu_done = sem("gelu_done")
        gate_done = sem("gate_done")
        acc_added = sem("acc_added")
        out_turned = sem("out_turned")
        ln_o = sem("ln_o")
        rstd_o = sem("rstd_o")
        applied_o = sem("applied_o")
        affine = sem("affine")
        ffn1_added = sem("ffn1_added")
        ffn2_added = sem("ffn2_added")
        stored = sem("stored")
        ln_m = sem("ln_m")
        rstd_m = sem("rstd_m")
        applied_m = sem("applied_m")
        xm_turned = sem("xm_turned")
        xm_split = sem("xm_split")
        inx_made = sem("inx_made")
        inz_made = sem("inz_made")
        xpad_made = sem("xpad_made")
        halo_set = sem("halo_set")
        z_read = sem("z_read")
        conv = sem("conv")
        x_tanhed = sem("x_tanhed")
        x_silu = sem("x_silu")
        z_silu = sem("z_silu")
        xdbl_made = sem("xdbl_made")
        xdbl_read = sem("xdbl_read")
        dt_made = sem("dt_made")
        dt_read = sem("dt_read")
        sp_act = sem("sp_act")
        sp_dve = sem("sp_dve")
        begun = sem("begun")
        bc_spread = sem("bc_spread")
        decay_made = sem("decay_made")
        drive_made = sem("drive_made")
        scanned = sem("scanned")
        seen_made = sem("seen_made")
        y_added = sem("y_added")
        carry_kept = sem("carry_kept")
        carry_moved = sem("carry_moved")
        y_gated = sem("y_gated")
        mamba_made = sem("mamba_made")
        mamba_added = sem("mamba_added")

        N_OF = {0: [], 1: [0], 2: [1], 3: [2], 4: [3, 4], 5: [5], 6: [6], 7: [7]}
        N_A = 8
        N_BEGIN, N_HIGH, N_X, N_XIN = 4, 10, 13, 14
        ROUTE = 23
        ROUTES = {0: range(10), 1: range(10, 16), 2: range(16, ROUTE)}
        ROUTES.update({e: () for e in range(3, E)})
        SPD = 6
        SPA = 5

        def parts(k):
            if not isinstance(k, int):
                return True, True
            return 0 <= k < CHUNKS, LAG <= k < UNITS

        def span(k):
            f1, f2 = parts(k)
            return (0 if f1 else TT), (2 * TT if f2 else TT)

        def chunk_ok(c):
            return not isinstance(c, int) or 0 <= c < CHUNKS

        def unit_ok(k):
            return not isinstance(k, int) or 0 <= k < UNITS

        def x_tile(k, j):
            at = TT * k + j if j < TT else TT * (k - LAG) + j - TT
            return xs[:, at, :] if isinstance(at, int) else xs[:, bass.ds(at, 1), :].rearrange("p a d -> p (a d)")

        def x_chunk(c):
            at = TT * c
            return xs[:, at:at + TT, :] if isinstance(at, int) else xs[:, bass.ds(at, TT), :]

        def over_units(eng, body):
            for k in range(LOOP[0]):
                body(k)
            with eng.Fori(*LOOP) as k:
                body(k)
            for k in range(LOOP[1], UNITS + 1):
                body(k)

        def bc_wide(n, half):
            return bc_bank[n % BB][:, half * CT:(half + 1) * CT].rearrange(
                "p (a t) -> p a t", a=1).to_broadcast([P, H, CT])

        block = ctx.enter_context(nc.Block())

        @block.sync
        def _(sp):
            def load_x(b, r, q0):
                dst = xs[:, :, :].rearrange("p (q b r) d -> p q b r d", b=NB, r=TT)[:, q0:, b, r]
                src = hidden[b].rearrange("(q r p) d -> p q r d", p=P, r=TT)[:, q0:, r]
                sp.dma_start(dst, src).then_inc(ld_x, 16)

            sp.dma_start(xs[:, 0:TT, :], hidden[0, 0:CT].rearrange("(r p) d -> p r d", p=P)).then_inc(ld_x0, 16)
            sp.dma_start(rows[0:NB1, :], b1.rearrange("e (m p) -> (e m) p", p=P)).then_inc(ld_vec, 16)
            for i, v in enumerate((conv_b, dt_b, d_par)):
                sp.dma_start(rows[NB1 + H * i:NB1 + H * i + H, :],
                             v.rearrange("(h p) -> h p", p=P)).then_inc(ld_vec, 16)
            sp.dma_start(bg_sb[:, :], bg.rearrange("(a e) -> a e", a=1).to_broadcast([P, E])).then_inc(ld_vec, 16)
            sp.dma_start(wg_in, Wg).then_inc(ld_vec, 16)
            for e in range(E):
                sp.dma_start(w1_in[e], W1[e]).then_inc(ld_w1[e], 16)
            sp.dma_start(win_in, in_w).then_inc(ld_mamba, 16)
            for e in range(E):
                sp.dma_start(w2[:, e], W2[e].rearrange("(m p) d -> p m d", p=P)).then_inc(ld_w2, 16)
            for b in range(NB):
                for r in range(TT):
                    load_x(b, r, 1 if b == 0 else 0)
            sp.dma_start(xp_sb[:, :, :], xp_w.rearrange("(h p) n -> p h n", p=P)).then_inc(ld_mamba, 16)
            sp.dma_start(dtw_sb[:, :], dt_w).then_inc(ld_mamba, 16)
            sp.dma_start(wout_sb[:, :, :], out_w.rearrange("(h p) n -> p h n", p=P)).then_inc(ld_mamba, 16)

            def gates(k):
                t0, t1 = span(k)
                c0, c1 = t0 * P, t1 * P
                wait(sp, cwT_made, k + 1)
                sp.dma_start(cw_dram[:, c0:c1], cwT[:, c0:c1]).then_inc(cw_stored, 16)
                wait(sp, gate_done, E * k)
                sp.wait_ge(cw_stored, 16 * k + 16)
                for i in range(E // SPREAD):
                    e0, e1 = SPREAD * i, SPREAD * i + SPREAD
                    src = cw_dram[e0:e1, c0:c1].rearrange("(a e) c -> a e c", a=1).to_broadcast([P, SPREAD, c1 - c0])
                    sp.dma_start(cwB[:, e0:e1, c0:c1], src).then_inc(cw_spread[i], 16)

            def store(q, b):
                rows_out = out[b].rearrange("(q p) d -> p q d", p=P)
                if isinstance(q, int):
                    c = NB * q + b
                    dst, src = rows_out[:, TT * q:TT * q + TT, :], xs[:, TT * c:TT * c + TT, :]
                else:
                    to = sp.snap(TT * q)
                    at = sp.snap(TT * NB * q + TT * b)
                    dst, src = rows_out[:, bass.ds(to, TT), :], xs[:, bass.ds(at, TT), :]
                sp.wait_ge(ffn2_added, NB * q + b + 1)
                sp.dma_start(dst, src).then_inc(stored, 16)

            for k in range(LAG + 1):
                gates(k)
            with sp.Fori(0, (CHUNKS - LAG - 1) // NB) as q:
                for b in range(NB):
                    gates(NB * q + LAG + 1 + b)
                    store(q, b)
            for c in range((CHUNKS - LAG - 1) // NB * NB, CHUNKS):
                if c + LAG + 1 < UNITS:
                    gates(c + LAG + 1)
                store(c // NB, c % NB)
            sp.wait_ge(stored, 16 * CHUNKS)

        @block.gpsimd
        def _(pool):
            g = nc.gpsimd
            g.memset(ident[:, :], 0.0).then_inc(pool_setup, 1)
            pool.wait_ge(pool_setup, 1)
            g.affine_select(out=ident[:, :], in_=ident[:, :], compare_op=ALU.not_equal, fill=1.0, base=0,
                            pattern=[[-1, P]], channel_multiplier=1).then_inc(ident_made, 1)
            g.memset(mhalf[:, :], -0.5)
            for i, value in enumerate((HALF_LN2, A1, B1)):
                g.memset(sp_bias[:, i:i + 1], value)
            g.memset(halo[:, :, :, :], 0.0)
            g.memset(carry[:, :, :, :], 0.0).then_inc(pool_setup, 1)
            pool.wait_ge(pool_setup, 2)

            def rstd(k, t0, t1, ve, rs, nm, needed, done):
                pool.wait_ge(needed, 3 * k + 3)
                g.tensor_tensor(rs[:, t0:t1], ve[:, t0:t1], mhalf[:, t0:t1], ALU.pow).then_inc(done, 1)
                pool.wait_ge(done, 2 * k + 1)
                g.tensor_tensor(nm[:, t0:t1], nm[:, t0:t1], rs[:, t0:t1], ALU.mult).then_inc(done, 1)

            def add_state(c, n):
                pool.wait_ge(seen_made, NS * c + n + 1)
                if n == 0:
                    wait(pool, carry_moved, 2 * c)
                    pool.wait_ge(begun, 2 * c + 1)
                else:
                    pool.wait_ge(y_added, NS * c + n)
                g.tensor_tensor(flat(y_acc[:, :, :]), flat(y_acc[:, :, :]), flat(seen[:, n % 2]),
                                ALU.add).then_inc(y_added, 1)
                g.tensor_copy(carry_new[:, :, n:n + 1], state[:, n % 2, :, CT - 1:CT]).then_inc(carry_kept, 1)

            def m_gate(c):
                pool.wait_ge(y_added, NS * c + NS)
                pool.wait_ge(begun, 2 * c + 2)
                g.tensor_tensor(flat(y_acc[:, :, :]), flat(y_acc[:, :, :]), flat(zs[:, :, :]), ALU.mult).then_inc(y_gated, 1)

            def z_times(c):
                pool.wait_ge(z_read, 2 * c + 2)
                g.tensor_tensor(z_tanh, z_tanh, flat(zs_next[:, :, :]), ALU.mult).then_inc(z_silu, 1)

            def z_plus(c):
                pool.wait_ge(z_silu, 2 * c + 1)
                g.tensor_tensor(flat(zs_next[:, :, :]), flat(zs_next[:, :, :]), z_tanh, ALU.add).then_inc(z_silu, 1)

            def add_expert(k, e):
                t0, t1 = span(k)
                c0, c1 = t0 * P, t1 * P
                pool.wait_ge(gate_done, E * k + e + 1)
                if e == 1:
                    wait(pool, out_turned, k)
                    if chunk_ok(k - 2):
                        pool.wait_ge(sp_dve, SPD * (k - 2) + SPD)
                    g.tensor_tensor(acc[:, c0:c1], gated[:, 0, c0:c1], gated[:, 1, c0:c1], ALU.add).then_inc(acc_added, 1)
                else:
                    pool.wait_ge(acc_added, ADDS * k + e - 1)
                    g.tensor_tensor(acc[:, c0:c1], acc[:, c0:c1], gated[:, e % 2, c0:c1], ALU.add).then_inc(acc_added, 1)

            def out_scale(k):
                t0, t1 = span(k)
                pool.wait_ge(applied_o, k + 1)
                if k_is0(k):
                    pool.wait_ge(scaled, 2)
                gb = gamma_h[:, :].rearrange("p (a d) -> p a d", a=1).to_broadcast([P, t1 - t0, D])
                g.tensor_tensor(on[:, t0:t1], on[:, t0:t1], gb, ALU.mult).then_inc(affine, 1)

            def out_shift(k):
                t0, t1 = span(k)
                bb = beta_h[:, :].rearrange("p (a d) -> p a d", a=1).to_broadcast([P, t1 - t0, D])
                pool.wait_ge(affine, 2 * k + 1)
                g.tensor_tensor(on[:, t0:t1], on[:, t0:t1], bb, ALU.add).then_inc(affine, 1)

            def k_is0(k):
                return isinstance(k, int) and k == 0

            def body(k):
                c1, c2, c3 = k - 1, k - 2, k - 3
                for e in range(E):
                    if chunk_ok(c3) and e < E - 1:
                        add_state(c3, N_A + e - 1)
                    if e == 1 and unit_ok(k - 1):
                        rstd(k - 1, *span(k - 1), o_ve, o_rs, o_nm, ln_o, rstd_o)
                    if e == 4 and unit_ok(k - 1):
                        out_scale(k - 1)
                    if e == 5 and unit_ok(k - 1):
                        out_shift(k - 1)
                    if chunk_ok(c2):
                        if e == 2:
                            z_times(c2)
                        if e == 3:
                            z_plus(c2)
                for e in range(E):
                    if e == 0 and chunk_ok(c1):
                        rstd(c1, 0, TT, m_ve, m_rs, m_nm, ln_m, rstd_m)
                    if e == 0 and chunk_ok(c3):
                        add_state(c3, NS - 2)
                        add_state(c3, NS - 1)
                        m_gate(c3)
                    if e >= 1 and unit_ok(k):
                        add_expert(k, e)
                    if chunk_ok(c2):
                        for n in N_OF[e]:
                            if n >= 1:
                                add_state(c2, n - 1)
                    if e == 3 and unit_ok(k + 1):
                        rstd(k + 1, *span(k + 1), f_ve, f_rs, f_nm, ln_f, rstd_f)

            rstd(0, *span(0), f_ve, f_rs, f_nm, ln_f, rstd_f)
            over_units(pool, body)

        @block.vector
        def _(dve):
            v = nc.vector

            for e in range(E):
                last = v.memset(rank[:, :, e:e + 1], float(E - e))
            last.then_inc(consts_made, 1)
            n_split = [0]

            def split(hi, lo, src):
                v.tensor_copy(hi, src).then_inc(split_made, 1)
                n_split[0] += 1
                dve.wait_ge(split_made, n_split[0])
                v.tensor_tensor(lo, src, hi.bitcast(F32), ALU.subtract).then_inc(split_made, 1)
                n_split[0] += 1

            def carry_wait():
                v.memset(spare[:, :], 0.0)

            def ln_stats(src, tiles, st, done, count):
                carry_wait()
                for j in tiles:
                    last = v.bn_stats(st[:, j, :], src(j))
                last.then_inc(done, 1)
                dve.wait_ge(done, count + 1)
                carry_wait()

            def ln_moments(tiles, st, mv, ve, nm, done, count):
                for j in tiles:
                    last = v.bn_aggr(mv[:, j, :], st[:, j, :])
                last.then_inc(done, 1)
                dve.wait_ge(done, count + 2)
                t0, t1 = tiles[0], tiles[-1] + 1
                v.tensor_scalar(nm[:, t0:t1], mv[:, t0:t1, 0:1].rearrange("p a b -> p (a b)"), -1.0, None, ALU.mult)
                v.tensor_scalar(ve[:, t0:t1], mv[:, t0:t1, 1:2].rearrange("p a b -> p (a b)"), EPS_LN, None,
                                ALU.add).then_inc(done, 1)

            def pre_norm(k):
                tiles = range(*span(k))
                if isinstance(k, int) and k == 0:
                    dve.wait_ge(ld_x0, 16)
                if isinstance(k, int) and k == 1:
                    dve.wait_ge(ld_x, 16 * NB * TT)
                if parts(k)[1]:
                    wait(dve, mamba_added, k - LAG + 1)
                ln_stats(lambda j: x_tile(k, j), tiles, f_st, ln_f, 3 * k)
                ln_moments(tiles, f_st, f_mv, f_ve, f_nm, ln_f, 3 * k)

            def pre_split(k):
                t0, t1 = span(k)
                c0, c1 = t0 * P, t1 * P
                dve.wait_ge(x_turned, k + 1)
                wait(dve, work_full, WORK * (k - 1) + E * M)
                if isinstance(k, int) and k == 0:
                    v.tensor_copy(x_hi[:, c0:c1], f_bank[:, c0:c1]).then_inc(x_split, 1)
                dve.wait_ge(x_split, 2 * k + 1)
                v.tensor_tensor(x_lo[:, c0:c1], f_bank[:, c0:c1], x_hi[:, c0:c1].bitcast(F32),
                                ALU.subtract).then_inc(x_split, 1)

            def router(k, i):
                t0, t1 = span(k)
                nt = t1 - t0
                cut = slice(t0, t1)

                def wide(t):
                    return t[:, cut].rearrange("p (a b) -> p a b", b=1).to_broadcast([P, nt, E])

                if i == 0:
                    dve.wait_ge(logits_made, k + 1)
                    bgw = bg_sb[:, :].rearrange("p (a e) -> p a e", a=1).to_broadcast([P, nt, E])
                    made = v.tensor_tensor(lg[:, cut], f_bank[:, t0 * E:t1 * E].rearrange("p (a e) -> p a e", e=E),
                                           bgw, ALU.add)
                    made.then_inc(route, 1)
                    return
                dve.wait_ge(route, ROUTE * k + i)
                if i == 1:
                    made = v.tensor_reduce(top[:, cut], lg[:, cut], AX, ALU.max)
                elif i == 2:
                    wait(dve, tanhs, k)
                    made = v.tensor_tensor(sh[:, cut], lg[:, cut], wide(top), ALU.subtract)
                elif i == 3:
                    made = v.tensor_tensor(eq[:, cut], lg[:, cut], wide(top), ALU.is_equal)
                elif i == 4:
                    made = v.tensor_tensor(eq[:, cut], eq[:, cut], rank[:, cut], ALU.mult)
                elif i == 5:
                    made = v.tensor_reduce(best[:, cut], eq[:, cut], AX, ALU.max)
                elif i == 6:
                    made = v.tensor_tensor(first[:, cut], eq[:, cut], wide(best), ALU.is_equal)
                elif i == 7:
                    made = v.scalar_tensor_tensor(lg2[:, cut], first[:, cut], FAR, lg[:, cut], ALU.mult, ALU.add)
                elif i == 8:
                    made = v.tensor_reduce(top[:, cut], lg2[:, cut], AX, ALU.max)
                elif i == 9:
                    made = v.tensor_tensor(eq[:, cut], lg2[:, cut], wide(top), ALU.is_equal)
                elif i == 10:
                    made = v.tensor_tensor(eq[:, cut], eq[:, cut], rank[:, cut], ALU.mult)
                elif i == 11:
                    made = v.tensor_reduce(best[:, cut], eq[:, cut], AX, ALU.max)
                elif i == 12:
                    made = v.tensor_tensor(both[:, cut], eq[:, cut], wide(best), ALU.is_equal)
                elif i == 13:
                    made = v.tensor_tensor(both[:, cut], both[:, cut], first[:, cut], ALU.add)
                elif i == 14:
                    dve.wait_ge(tanhs, k + 1)
                    made = v.tensor_scalar(eq[:, cut], ex[:, cut], -1.0, 1.0, ALU.mult, ALU.add)
                elif i == 15:
                    made = v.reciprocal(eq[:, cut], eq[:, cut])
                elif i == 16:
                    made = v.scalar_tensor_tensor(ex[:, cut], ex[:, cut], 1.0, eq[:, cut], ALU.add, ALU.mult)
                elif i == 17:
                    made = v.tensor_tensor(num[:, cut], ex[:, cut], both[:, cut], ALU.mult)
                elif i == 18:
                    made = v.tensor_reduce(whole[:, cut], ex[:, cut], AX, ALU.add)
                elif i == 19:
                    made = v.tensor_reduce(den[:, cut], num[:, cut], AX, ALU.add)
                elif i == 20:
                    made = v.scalar_tensor_tensor(den[:, cut], whole[:, cut], EPS_GATE, den[:, cut], ALU.mult, ALU.add)
                elif i == 21:
                    made = v.reciprocal(den[:, cut], den[:, cut])
                else:
                    wait(dve, cw_turned, k)
                    made = v.tensor_tensor(cw[:, cut], num[:, cut], wide(den), ALU.mult)
                made.then_inc(route, 1)

            def gate(k, e):
                t0, t1 = span(k)
                c0, c1 = t0 * P, t1 * P
                dve.wait_ge(work_full, WORK * k + E * M + e + 1)
                if e % SPREAD == 0:
                    dve.wait_ge(cw_spread[e // SPREAD], 16 * k + 16)
                if e == 0 and chunk_ok(k - 2):
                    dve.wait_ge(z_silu, 2 * (k - 2) + 2)
                wait(dve, acc_added, ADDS * k + (max(1, e - 2) if e >= 2 else 0))
                v.tensor_tensor(gated[:, e % 2, c0:c1], work[e % WB][:, c0:c1], cwB[:, e, c0:c1],
                                ALU.mult).then_inc(gate_done, 1)

            def out_norm(k):
                tiles = range(*span(k))
                dve.wait_ge(out_turned, k + 1)
                ln_stats(lambda j: f_bank[:, j * D:(j + 1) * D], tiles, o_st, ln_o, 3 * k)
                ln_moments(tiles, o_st, o_mv, o_ve, o_nm, ln_o, 3 * k)

            def out_add(k):
                f1, f2 = parts(k)
                dve.wait_ge(affine, 2 * k + 2)
                if f1:
                    v.tensor_tensor(x_chunk(k), x_chunk(k), on[:, 0:TT], ALU.add).then_inc(ffn1_added, 1)
                if f2:
                    v.tensor_tensor(x_chunk(k - LAG), x_chunk(k - LAG), on[:, TT:2 * TT], ALU.add).then_inc(ffn2_added, 1)

            def m_tile(c):
                return lambda j: x_tile(c, j)

            def m_norm(c):
                dve.wait_ge(ffn1_added, c + 1)
                ln_stats(m_tile(c), range(TT), m_st, ln_m, 3 * c)
                ln_moments(range(TT), m_st, m_mv, m_ve, m_nm, ln_m, 3 * c)

            def m_split(c):
                dve.wait_ge(xm_turned, c + 1)
                wait(dve, inz_made, c)
                dve.wait_ge(xm_split, 2 * c + 1)
                v.tensor_tensor(xm_lo[:, :], m_bank[:, 0:CT], xm_hi[:, :].bitcast(F32), ALU.subtract).then_inc(xm_split, 1)

            def m_halo(c):
                dve.wait_ge(xpad_made, c + 1)
                v.tensor_copy(xpad[:, :, 0:KC - 1], halo[:, 0]).then_inc(halo_set, 1)
                dve.wait_ge(halo_set, 3 * c + 1)
                v.tensor_copy(halo[:, 0], halo[:, 1]).then_inc(halo_set, 1)
                dve.wait_ge(halo_set, 3 * c + 2)
                v.tensor_copy(halo[:, 1], xpad[:, :, CT:CT + KC - 1]).then_inc(halo_set, 1)

            def m_carry(c):
                dve.wait_ge(carry_kept, NS * c + NS)
                v.tensor_copy(carry[:, 0], carry[:, 1]).then_inc(carry_moved, 1)
                dve.wait_ge(carry_moved, 2 * c + 1)
                v.tensor_copy(carry[:, 1], carry_new[:, :, :]).then_inc(carry_moved, 1)

            def m_conv(c, routes=()):
                for t in range(KC - 1):
                    for step in routes[2 * t:2 * t + 1]:
                        router(*step)
                    dve.wait_ge(conv, KC * c + t + 1)
                    for h in range(H):
                        last = v.scalar_tensor_tensor(u[:, h], xpad[:, h, t:t + CT], convw_sb[:, h, t:t + 1],
                                                      u[:, h], ALU.mult, ALU.add)
                        if h == 0:
                            for step in routes[2 * t + 1:2 * t + 2]:
                                router(*step)
                    last.then_inc(conv, 1)

            def m_silu(c):
                dve.wait_ge(x_tanhed, c + 1)
                a = flat(u[:, :, :])
                v.scalar_tensor_tensor(a, x_tanh, 1.0, a, ALU.add, ALU.mult).then_inc(x_silu, 1)

            def m_xdbl(c):
                dve.wait_ge(xdbl_read, 3 * c + 2)
                v.tensor_tensor(bc[2 * NS:4 * NS, :], m_bank[R:R + 2 * NS, 0:CT],
                                bc[0:2 * NS, :].bitcast(F32), ALU.subtract).then_inc(xdbl_read, 1)

            def m_s4(c):
                dve.wait_ge(sp_act, SPA * c + 2)
                v.scalar_tensor_tensor(sp_s4, sp_tanh, 1.0, sp_exp, ALU.add, ALU.mult).then_inc(sp_dve, 1)

            def m_softplus(c):
                base = [SPD * c + 1]

                def step(ins):
                    ins.then_inc(sp_dve, 1)
                    base[0] = base[0] + 1
                    dve.wait_ge(sp_dve, base[0])

                dve.wait_ge(sp_act, SPA * c + 4)
                step(v.tensor_scalar(sp_b, sp_b, LEAD / 4, B0 * LEAD / 4, ALU.mult, ALU.add))
                dve.wait_ge(sp_act, SPA * c + 5)
                step(v.scalar_tensor_tensor(sp_b, sp_a, A0, sp_b, ALU.add, ALU.mult))
                step(v.tensor_tensor(sp_b, sp_b, sp_s4, ALU.mult))
                dve.wait_ge(dt_read, 2 * c + 2)
                step(v.tensor_tensor(dt[:, :, :], sp_b, sp_pos, ALU.add))
                v.tensor_tensor(flat(dtu[:, :, :]), flat(dt[:, :, :]), flat(u[:, :, :]), ALU.mult).then_inc(sp_dve, 1)

            def m_state(c, n, routes=()):
                if n < NS:
                    dve.wait_ge(bc_spread, NS * c + n + 1)
                    if n == 0:
                        dve.wait_ge(sp_dve, SPD * c + SPD)
                    if n >= 2:
                        dve.wait_ge(scanned, NS * c + n - 1)
                    v.tensor_tensor(drive[:, n % 2], dtu[:, :, :], bc_wide(n, 0), ALU.mult).then_inc(drive_made, 1)
                for step in routes[0:1]:
                    router(*step)
                if n >= 1:
                    dve.wait_ge(scanned, NS * c + n)
                    wait(dve, y_added, NS * c + n - 2)
                    v.tensor_tensor(seen[:, (n - 1) % 2], state[:, (n - 1) % 2], bc_wide(n - 1, 1),
                                    ALU.mult).then_inc(seen_made, 1)
                for step in routes[1:2]:
                    router(*step)
                if n < NS:
                    dve.wait_ge(drive_made, NS * c + n + 1)
                    dve.wait_ge(decay_made, NS * c + n + 1)
                    wait(dve, carry_kept, NS * c + n - 1)
                    if n >= 2:
                        dve.wait_ge(seen_made, NS * c + n - 1)
                    if n == 0:
                        wait(dve, carry_moved, 2 * c)
                    for h in range(H):
                        last = v.tensor_tensor_scan(state[:, n % 2, h], decay[:, n % NSLOT, h], drive[:, n % 2, h],
                                                    carry[:, 0, h, n:n + 1], ALU.mult, ALU.add)
                        if h == 0:
                            for step in routes[2:3]:
                                router(*step)
                    last.then_inc(scanned, 1)
                for step in routes[3:]:
                    router(*step)

            def m_add(c):
                dve.wait_ge(mamba_made, c + 1)
                v.tensor_tensor(x_chunk(c), x_chunk(c), m_bank[:, 0:TT * D].rearrange("p (a d) -> p a d", d=D),
                                ALU.add).then_inc(mamba_added, 1)

            dve.wait_ge(ld_vec, 16 * 6)
            split(wg_hi[:, :], wg_lo[:, :], wg_in)
            pre_norm(0)
            dve.wait_ge(consts_made, 1)
            dve.wait_ge(pool_setup, 2)
            dve.wait_ge(cols_turned, 1)
            v.tensor_copy(cols[:, :], m_bank[:, 0:ROWS]).then_inc(cols_made, 1)
            for e in range(E):
                if e == 1:
                    pre_split(0)
                if e == 3:
                    for i in range(14):
                        router(0, i)
                dve.wait_ge(ld_w1[e], 16)
                split(w1_hi[:, e], w1_lo[:, e], w1_in[e])
            for i in range(14, ROUTE):
                router(0, i)
            dve.wait_ge(ld_mamba, 16 * 8)
            split(win_hi[:, :], win_lo[:, :], win_in)
            dve.wait_ge(cols_made, 1)
            v.tensor_scalar(convb_col, convb_col, 0.5, None, ALU.mult)
            v.tensor_scalar(flat(convw_sb[:, :, :]), flat(convw_sb[:, :, :]), 0.5, None, ALU.mult)
            v.tensor_scalar(gamma_h[:, :], gamma_h[:, :], 0.5, None, ALU.mult).then_inc(scaled, 1)
            v.tensor_scalar(beta_h[:, :], beta_h[:, :], 0.5, None, ALU.mult).then_inc(scaled, 1)
            dve.wait_ge(ident_made, 1)
            v.tensor_copy(pick[0:2 * NS, :], ident[0:2 * NS, 0:2 * NS])
            v.tensor_copy(pick[2 * NS:4 * NS, :], ident[2 * NS:4 * NS, 2 * NS:4 * NS]).then_inc(cols_made, 1)
            def body(k):
                c1, c2, c3 = k - 1, k - 2, k - 3
                for e in range(E):
                    routes = [(k, i) for i in ROUTES[e]] if unit_ok(k) and not (isinstance(k, int) and k == 0) else []
                    state_routes, other_routes = routes[:4], routes[4:]
                    if chunk_ok(c2):
                        if e == 4:
                            m_silu(c2)
                        if e == 7:
                            m_xdbl(c2)
                    if chunk_ok(c3) and e < E - 1:
                        m_state(c3, N_A + e, state_routes)
                    else:
                        for step in state_routes:
                            router(*step)
                    if e == 0 and chunk_ok(c2):
                        m_halo(c2)
                        m_conv(c2, other_routes)
                    else:
                        for step in other_routes:
                            router(*step)
                    if e == 1 and unit_ok(k - 1):
                        out_norm(k - 1)
                    if e == 6 and unit_ok(k - 1):
                        out_add(k - 1)
                if chunk_ok(c1):
                    m_norm(c1)
                if chunk_ok(c3):
                    m_state(c3, NS - 1)
                if chunk_ok(c2):
                    m_s4(c2)
                if chunk_ok(c3):
                    m_state(c3, NS)
                for e in range(E):
                    if unit_ok(k):
                        gate(k, e)
                    if e == 0 and chunk_ok(c2):
                        m_softplus(c2)
                    if e == 1:
                        if chunk_ok(c3):
                            m_carry(c3)
                    if e == 3 and chunk_ok(c3):
                        m_add(c3)
                    if e == 4 and chunk_ok(c1):
                        m_split(c1)
                    if unit_ok(k + 1):
                        if e == 3:
                            pre_norm(k + 1)
                        if e == 6:
                            pre_split(k + 1)
                    if chunk_ok(c2):
                        for n in N_OF[e]:
                            m_state(c2, n)

            over_units(dve, body)

        @block.scalar
        def _(act):
            s = nc.scalar
            act.dma_start(gamma_h[:, :], gamma.rearrange("(a e) -> a e", a=1).to_broadcast([P, D])).then_inc(ld_mamba, 16)
            act.dma_start(beta_h[:, :], beta.rearrange("(a e) -> a e", a=1).to_broadcast([P, D])).then_inc(ld_mamba, 16)
            act.dma_start(a_neg[:, :, :], a_log.rearrange("(h p) n -> p h n", p=P)).then_inc(ld_mamba, 16)
            act.dma_start(convw_sb[:, :, :], conv_w.rearrange("(h p) n -> p h n", p=P)).then_inc(ld_mamba, 16)
            act.dma_start(b2_sb[:, :], b2).then_inc(ld_w2, 16)
            act.wait_ge(cols_made, 1)

            def gelu(k, e, m):
                t0, t1 = span(k)
                c0, c1 = t0 * P, t1 * P
                i = e * M + m
                act.wait_ge(work_full, WORK * k + i + 1)
                if isinstance(k, int) and k == 0 and i == STAGED:
                    act.wait_ge(split_made, 2 * (E + 2))
                s.activation(hid[:, i, c0:c1], work[i % WB][:, c0:c1], ACT.Gelu,
                             bias=b1_col[:, i:i + 1]).then_inc(gelu_done, 1)

            def ln_apply(src, dst, tiles, rs, nm, done):
                for j in tiles:
                    last = s.activation(dst[:, j, :], src(j), ACT.Identity, scale=rs[:, j:j + 1], bias=nm[:, j:j + 1])
                last.then_inc(done, 1)

            def pre_apply(k):
                act.wait_ge(rstd_f, 2 * k + 2)
                wait(act, x_turned, k)
                ln_apply(lambda j: x_tile(k, j), xn, range(*span(k)), f_rs, f_nm, applied_f)

            def out_apply(k):
                act.wait_ge(rstd_o, 2 * k + 2)
                ln_apply(lambda j: f_bank[:, j * D:(j + 1) * D], on, range(*span(k)), o_rs, o_nm, applied_o)

            def m_apply(c):
                act.wait_ge(rstd_m, 2 * c + 2)
                wait(act, dt_made, c)
                ln_apply(lambda j: x_tile(c, j), xm, range(TT), m_rs, m_nm, applied_m)

            def cw_copy(k):
                t0, t1 = span(k)
                c0, c1 = t0 * P, t1 * P
                act.wait_ge(cw_turned, k + 1)
                wait(act, cw_stored, 16 * k)
                wait(act, out_turned, k)
                s.activation(cwT[:, c0:c1], f_bank[0:E, c0:c1], ACT.Copy).then_inc(cwT_made, 1)

            def softmax_tanh(k):
                t0, t1 = span(k)
                act.wait_ge(route, ROUTE * k + 3)
                s.activation(ex[:, t0:t1], sh[:, t0:t1], ACT.Tanh, scale=0.5).then_inc(tanhs, 1)

            def m_xin(c):
                act.wait_ge(inx_made, c + 1)
                wait(act, conv, KC * c)
                wait(act, halo_set, 3 * c)
                wait(act, sp_dve, SPD * c)
                s.activation(xpad[:, :, KC - 1:], m_bank[:, :].rearrange("p (h t) -> p h t", h=H),
                             ACT.Copy).then_inc(xpad_made, 1)
                for h in range(H):
                    last = s.activation(u[:, h], m_bank[:, h * CT:(h + 1) * CT], ACT.Identity,
                                        scale=convw_sb[:, h, KC - 1:KC], bias=convb_col[:, h:h + 1])
                last.then_inc(conv, 1)

            def m_zin(c):
                act.wait_ge(inz_made, c + 1)
                wait(act, begun, 2 * c)
                s.activation(flat(zs_next[:, :, :]), m_bank[:, :], ACT.Copy, scale=0.5).then_inc(z_read, 1)
                wait(act, acc_added, ADDS * (c + 2))
                s.activation(z_tanh, m_bank[:, :], ACT.Tanh, scale=0.5).then_inc(z_read, 1)

            def m_xtanh(c):
                act.wait_ge(conv, KC * c + KC)
                s.activation(x_tanh, flat(u[:, :, :]), ACT.Tanh).then_inc(x_tanhed, 1)

            def m_xdbl(c):
                act.wait_ge(xdbl_made, c + 1)
                s.activation(dt_low, m_bank[0:R, 0:CT], ACT.Copy).then_inc(xdbl_read, 1)
                wait(act, bc_spread, NS * c)
                s.activation(bc[0:2 * NS, :], m_bank[R:R + 2 * NS, 0:CT], ACT.Copy).then_inc(xdbl_read, 1)

            def m_pre(c):
                act.wait_ge(dt_made, c + 1)
                if isinstance(c, int) and c == 0:
                    act.wait_ge(pool_setup, 2)
                act.wait_ge(out_turned, c + 2)
                for h in range(H):
                    src = m_bank[:, h * CT:(h + 1) * CT]
                    last = s.activation(sp_abs[:, h], src, ACT.Abs, bias=dtb_col[:, h:h + 1])
                last.then_inc(dt_read, 1)

            def m_softplus(c):
                act.wait_ge(dt_read, 2 * c + 1)
                f1, f2 = parts(c + 1)
                if f2:
                    act.wait_ge(ffn2_added, c + 2 - LAG)
                else:
                    act.wait_ge(ffn1_added, c + 2)
                s.activation(sp_exp, sp_abs, ACT.Exp, scale=-1.0).then_inc(sp_act, 1)
                s.activation(sp_tanh, sp_abs, ACT.Tanh, scale=0.5, bias=sp_bias[:, 0:1]).then_inc(sp_act, 1)

            def m_squares(c):
                act.wait_ge(sp_dve, SPD * c + 1)
                s.activation(sp_sq, sp_s4, ACT.Square, scale=0.25).then_inc(sp_act, 1)
                act.wait_ge(sp_act, SPA * c + 3)
                s.activation(sp_b, sp_sq, ACT.Square, bias=sp_bias[:, 2:3]).then_inc(sp_act, 1)
                s.activation(sp_a, sp_sq, ACT.Square, bias=sp_bias[:, 1:2]).then_inc(sp_act, 1)
                for h in range(H):
                    src = m_bank[:, h * CT:(h + 1) * CT]
                    last = s.activation(sp_pos[:, h], src, ACT.Relu, bias=dtb_col[:, h:h + 1])
                last.then_inc(dt_read, 1)

            def m_begin(c):
                act.wait_ge(z_silu, 2 * c + 2)
                wait(act, mamba_made, c)
                for h in range(H):
                    last = s.activation(y_acc[:, h], u[:, h], ACT.Copy, scale=dpar_col[:, h:h + 1])
                last.then_inc(begun, 1)
                s.activation(flat(zs[:, :, :]), flat(zs_next[:, :, :]), ACT.Copy).then_inc(begun, 1)

            def x_high(k):
                t0, t1 = span(k)
                c0, c1 = t0 * P, t1 * P
                act.wait_ge(x_turned, k + 1)
                wait(act, work_full, WORK * (k - 1) + E * M)
                s.activation(x_hi[:, c0:c1], f_bank[:, c0:c1], ACT.Copy).then_inc(x_split, 1)

            def m_high(c):
                act.wait_ge(xm_turned, c + 1)
                wait(act, inz_made, c)
                s.activation(xm_hi[:, :], m_bank[:, 0:CT], ACT.Copy).then_inc(xm_split, 1)

            def decays(c, n):
                if isinstance(c, int) and c == 0 and n == 0:
                    act.wait_ge(a_made, 2)
                if n == 0:
                    act.wait_ge(sp_dve, SPD * c + SPD - 1)
                wait(act, scanned, NS * c + n - NSLOT + 1)
                for h in range(H):
                    last = s.activation(decay[:, n % NSLOT, h], dt[:, h], ACT.Exp, scale=a_neg[:, h, n:n + 1])
                last.then_inc(decay_made, 1)

            def body(k):
                c1, c2, c3 = k - 1, k - 2, k - 3
                for e in range(E):
                    for m in range(M):
                        if unit_ok(k):
                            gelu(k, e, m)
                        if e == E - 1 and m == 0 and chunk_ok(c2):
                            m_xdbl(c2)
                    if e == 0 and unit_ok(k):
                        softmax_tanh(k)
                    if e == 3 and unit_ok(k - 1):
                        out_apply(k - 1)
                    if e == 5 and unit_ok(k):
                        cw_copy(k)
                    if chunk_ok(c2):
                        if e == 1:
                            m_zin(c2)
                        if e == 2:
                            m_xtanh(c2)
                if isinstance(k, int) and k == 0:
                    act.wait_ge(ld_mamba, 16 * 8)
                    s.activation(flat(a_neg[:, :, :]), flat(a_neg[:, :, :]), ACT.Exp).then_inc(a_made, 1)
                    act.wait_ge(a_made, 1)
                    s.activation(flat(a_neg[:, :, :]), flat(a_neg[:, :, :]), ACT.Copy, scale=-1.0).then_inc(a_made, 1)
                if chunk_ok(c3):
                    decays(c3, NS - 1)
                if chunk_ok(c2):
                    m_pre(c2)
                    m_softplus(c2)
                    m_squares(c2)
                    for n in range(N_BEGIN):
                        decays(c2, n)
                    m_begin(c2)
                if chunk_ok(c1):
                    m_apply(c1)
                if chunk_ok(c2):
                    for n in range(N_BEGIN, N_HIGH):
                        decays(c2, n)
                if chunk_ok(c1):
                    m_high(c1)
                if unit_ok(k + 1):
                    pre_apply(k + 1)
                if chunk_ok(c2):
                    for n in range(N_HIGH, N_X):
                        decays(c2, n)
                if unit_ok(k + 1):
                    x_high(k + 1)
                if chunk_ok(c2):
                    for n in range(N_X, N_XIN):
                        decays(c2, n)
                if chunk_ok(c1):
                    m_xin(c1)
                if chunk_ok(c2):
                    for n in range(N_XIN, NS - 1):
                        decays(c2, n)

            pre_apply(0)
            over_units(act, body)

        @block.tensor
        def _(pe):
            t = nc.tensor

            def three(dst, hi_w, lo_w, hi_x, lo_x):
                t.matmul(dst, hi_w, hi_x, start=True, stop=False)
                t.matmul(dst, hi_w, lo_x, start=False, stop=False)
                return t.matmul(dst, lo_w, hi_x, start=False, stop=True)

            def last_use(uses, i):
                return max(j for j in range(uses) if j % WB == i)

            def turn_x(k):
                pe.wait_ge(applied_f, k + 1)
                wait(pe, cwT_made, k)
                for j in range(*span(k)):
                    last = t.transpose(f_bank[:, j * P:(j + 1) * P], xn[:, j, :], ident[:, :])
                last.then_inc(x_turned, 1)

            def logits(k):
                pe.wait_ge(x_split, 2 * k + 2)
                for j in range(*span(k)):
                    xh, xl = x_hi[:, j * P:(j + 1) * P], x_lo[:, j * P:(j + 1) * P]
                    dst = f_bank[:, j * E:(j + 1) * E]
                    t.matmul(dst, xh, wg_hi[:, :], start=True, stop=False)
                    t.matmul(dst, xh, wg_lo[:, :], start=False, stop=False)
                    last = t.matmul(dst, xl, wg_hi[:, :], start=False, stop=True)
                last.then_inc(logits_made, 1)

            def turn_cw(k):
                pe.wait_ge(route, ROUTE * k + ROUTE)
                wait(pe, applied_o, k)
                for j in range(*span(k)):
                    last = t.transpose(f_bank[0:E, j * P:(j + 1) * P], cw[:, j, :], ident[:, :])
                last.then_inc(cw_turned, 1)

            def w1(k, e, m):
                t0, t1 = span(k)
                c0, c1 = t0 * P, t1 * P
                i = e * M + m
                if isinstance(k, int) and k == 0 and m == 0:
                    pe.wait_ge(split_made, 2 * (e + 2))
                if i < WB:
                    wait(pe, gate_done, E * (k - 1) + last_use(E, i) + 1)
                else:
                    pe.wait_ge(gelu_done, E * M * k + i - WB + 1)
                cut = slice(m * P, (m + 1) * P)
                three(work[i % WB][:, c0:c1], w1_hi[:, e, cut], w1_lo[:, e, cut],
                      x_hi[:, c0:c1], x_lo[:, c0:c1]).then_inc(work_full, 1)

            def w2_(k, e):
                t0, t1 = span(k)
                c0, c1 = t0 * P, t1 * P
                if e < WB:
                    pe.wait_ge(gelu_done, E * M * k + last_use(E * M, e) + 1)
                else:
                    pe.wait_ge(gate_done, E * k + e - WB + 1)
                if isinstance(k, int) and k == 0 and e == 0:
                    pe.wait_ge(ld_w2, 16 * (E + 1))
                for m in range(M):
                    last = t.matmul(work[e % WB][:, c0:c1], w2[:, e, m, :], hid[:, e * M + m, c0:c1],
                                    start=m == 0, stop=m == M - 1)
                last.then_inc(work_full, 1)

            def turn_out(k):
                pe.wait_ge(acc_added, ADDS * k + ADDS)
                if unit_ok(k + 1):
                    pe.wait_ge(route, ROUTE * (k + 1) + 1)
                for j in range(*span(k)):
                    dst = f_bank[:, j * D:(j + 1) * D]
                    t.matmul(dst, acc[:, j * P:(j + 1) * P], ident[:, :], start=True, stop=False)
                    last = t.matmul(dst, cwT[:, j * P:(j + 1) * P], b2_sb[:, :], start=False, stop=True)
                last.then_inc(out_turned, 1)

            def turn_xm(c):
                pe.wait_ge(applied_m, c + 1)
                wait(pe, mamba_added, c - 1)
                for j in range(TT):
                    last = t.transpose(m_bank[:, j * P:(j + 1) * P], xm[:, j, :], ident[:, :])
                last.then_inc(xm_turned, 1)

            def in_proj(c, z, done):
                pe.wait_ge(xm_split, 2 * c + 2)
                if z:
                    pe.wait_ge(conv, KC * c + 1)
                for h in range(H):
                    at = z * DI + h * P
                    last = three(m_bank[:, h * CT:(h + 1) * CT], win_hi[:, at:at + P], win_lo[:, at:at + P],
                                 xm_hi[:, :], xm_lo[:, :])
                last.then_inc(done, 1)

            def x_proj(c):
                pe.wait_ge(x_silu, c + 1)
                pe.wait_ge(z_read, 2 * c + 2)
                for h in range(H):
                    last = t.matmul(m_bank[0:R + 2 * NS, 0:CT], xp_sb[:, h, :], u[:, h, :], start=h == 0, stop=h == H - 1)
                last.then_inc(xdbl_made, 1)

            def dt_proj(c):
                pe.wait_ge(xdbl_read, 3 * c + 3)
                for h in range(H):
                    last = t.matmul(m_bank[:, h * CT:(h + 1) * CT], dtw_sb[:, h * P:(h + 1) * P], dt_low,
                                    start=True, stop=True)
                last.then_inc(dt_made, 1)

            def spread(c, n):
                pe.wait_ge(xdbl_read, 3 * c + 3)
                wait(pe, seen_made, NS * c + max(n - BB + 1, 0))
                bank = bc_bank[n % BB]
                for i, row in enumerate((n, NS + n)):
                    one = pick[:, row:row + 1].to_broadcast([4 * NS, P])
                    last = t.matmul(bank[:, i * CT:(i + 1) * CT], one, bc[:, :], start=True, stop=True)
                last.then_inc(bc_spread, 1)

            def out_proj(c):
                pe.wait_ge(y_gated, c + 1)
                if chunk_ok(c + 1):
                    pe.wait_ge(dt_read, 2 * (c + 1) + 2)
                for j in range(TT):
                    for h in range(H):
                        last = t.matmul(m_bank[:, j * D:(j + 1) * D], y_acc[:, h, j * P:(j + 1) * P], wout_sb[:, h, :],
                                        start=h == 0, stop=h == H - 1)
                last.then_inc(mamba_made, 1)

            pe.wait_ge(ident_made, 1)
            pe.wait_ge(ld_vec, 16 * 6)
            t.transpose(m_bank[:, 0:ROWS], rows, ident[0:ROWS, 0:ROWS]).then_inc(cols_turned, 1)
            turn_x(0)
            logits(0)

            def body(k):
                c1, c2, c3 = k - 1, k - 2, k - 3
                for e in range(E):
                    if e == 5 and unit_ok(k):
                        turn_cw(k)
                    if e == 0 and chunk_ok(c3):
                        spread(c3, N_A)
                    for m in range(M):
                        if unit_ok(k):
                            w1(k, e, m)
                        if m == 0 and e >= 1 and chunk_ok(c3):
                            spread(c3, N_A + e)
                    if e == 1 and unit_ok(k - 1):
                        turn_out(k - 1)
                    if not chunk_ok(c2):
                        continue
                    if e == 0:
                        in_proj(c2, 1, inz_made)
                    if e == 5:
                        x_proj(c2)
                    if e == 7:
                        dt_proj(c2)
                for e in range(E):
                    if unit_ok(k):
                        w2_(k, e)
                    if e == 2 and chunk_ok(c3):
                        out_proj(c3)
                    if chunk_ok(c2):
                        if e == 1:
                            pe.wait_ge(cols_made, 2)
                        for n in N_OF[e]:
                            spread(c2, n)
                    if chunk_ok(c1):
                        if e == 4:
                            turn_xm(c1)
                        if e == 6:
                            in_proj(c1, 0, inx_made)
                    if e == 5 and unit_ok(k + 1):
                        turn_x(k + 1)
                    if e == 7 and unit_ok(k + 1):
                        logits(k + 1)

            over_units(pe, body)


_INS = ["L0_attn_hidden_states", "L0_attn_in_proj_w", "L0_attn_conv_w", "L0_attn_conv_b", "L0_attn_x_proj_w",
        "L0_attn_dt_proj_w", "L0_attn_dt_bias", "L0_attn_A_log", "L0_attn_D_param", "L0_attn_out_proj_w",
        "L0_ffn_Wg", "L0_ffn_bg", "L0_ffn_W1", "L0_ffn_b1", "L0_ffn_W2", "L0_ffn_b2", "L0_ffn_gamma", "L0_ffn_beta"]


def kernel(**inputs):
    import numpy as np
    import concourse.bacc as bacc
    from concourse.bass_utils import run_bass_kernel_spmd

    nc = bacc.Bacc("TRN2", target_bir_lowering=False, num_devices=1)
    arrays, args = {}, []
    for name in _INS:
        a = np.ascontiguousarray(inputs[name])
        arrays[f"in_{name}"] = a
        args.append(nc.dram_tensor(f"in_{name}", a.shape, mybir.dt.from_np(a.dtype), kind="ExternalInput").ap())
    experts = arrays["in_L0_ffn_W1"].shape[0]
    args.append(nc.dram_tensor("gate_scratch", (experts, 2 * CT), F32, kind="Internal").ap())
    shape = arrays["in_L0_attn_hidden_states"].shape
    args.append(nc.dram_tensor("out", shape, F32, kind="ExternalOutput").ap())
    macaron(nc, *args)
    return run_bass_kernel_spmd(nc, [arrays], core_ids=[0]).results[0]["out"]
```
